# Optimizing a Trainium2 kernel written in Bass

```python
import numpy as np
import jax
import jax.numpy as jnp

def _softmax(x, axis=-1):
    return jax.nn.softmax(x, axis=axis)

def _gelu(x):
    return jax.nn.gelu(x, approximate=True)

def _silu(x):
    return jax.nn.silu(x)

def _sigmoid(x):
    return jax.nn.sigmoid(x)

def _layernorm(x, axis=-1, eps=1e-05):
    m = jnp.mean(x, axis=axis, keepdims=True)
    v = jnp.var(x, axis=axis, keepdims=True)
    return (x - m) / jnp.sqrt(v + eps)

def _scatter_add(tgt, idx, src, axis=0):
    return tgt.at[idx].add(src)

def _segment_sum(src, seg, n):
    return jax.ops.segment_sum(src, seg, n)
kernel_name = 'mk_xattn_ffn_d1_seqx_r4_99e47b'

def setup_inputs(seed: int=0):
    np.random.seed(seed)
    _w = jnp.asarray

    def _rec_inputs():
        import jax
        import jax.numpy as jnp
        _rk = jax.random.key(seed)
        x = -0.0002928 + 1 * jax.random.normal(jax.random.fold_in(_rk, 1), (8, 512, 256), jnp.float32)
        _lenS = 512 - jax.random.randint(jax.random.fold_in(_rk, 7), (8,), 0, max(1, 512 // 4) + 1, jnp.int32)
        _lenS2 = 1024 - jax.random.randint(jax.random.fold_in(_rk, 8), (8,), 0, max(1, 1024 // 4) + 1, jnp.int32)
        _ctx_512P = jax.random.normal(jax.random.fold_in(_rk, 11), (8, 16, 128), jnp.float32)
        _ctx_512c = jax.random.dirichlet(jax.random.fold_in(_rk, 511), 0.3 * jnp.ones((16,), jnp.float32), (8, 1024))
        _ctx_512t = jnp.einsum('bsk,bkd->bsd', _ctx_512c, _ctx_512P)
        _ctx_512t = _ctx_512t * jax.lax.rsqrt(jnp.mean(jnp.square(_ctx_512t)) + 1e-12) * 0.953939
        ctx_512 = 0.00222621 + 0.99962 * (_ctx_512t + 0.3 * jax.random.normal(jax.random.fold_in(_rk, 611), (8, 1024, 128), jnp.float32))
        return (x, ctx_512)
    x, ctx_512 = _rec_inputs()

    def _L0_xattn_setup():
        import jax, jax.numpy as jnp
        import numpy as np
        B, T, TC, C, CC, H = (2, 512, 128, 256, 128, 16)
        D = C // H

        def _heads(t):
            b, l, _ = t.shape
            return t.reshape(b, l, H, D).transpose(0, 2, 1, 3)
        key = jax.random.key(seed)
        ks = jax.random.split(key, 18)
        w = lambda k, i, o: jax.random.normal(k, (i, o), jnp.float32) / np.sqrt(i).astype(np.float32)
        return {'x': jax.random.normal(ks[0], (B, T, C), jnp.float32), 'cross_input': jax.random.normal(ks[1], (B, TC, CC), jnp.float32), 'Wk': w(ks[2], C, C), 'bk': jnp.zeros((C,), jnp.float32), 'Wq': w(ks[3], C, C), 'bq': jnp.zeros((C,), jnp.float32), 'Wv': w(ks[4], C, C), 'bv': jnp.zeros((C,), jnp.float32), 'Wck': w(ks[5], CC, C), 'bck': jnp.zeros((C,), jnp.float32), 'Wcq': w(ks[6], C, C), 'bcq': jnp.zeros((C,), jnp.float32), 'Wcv': w(ks[7], CC, C), 'bcv': jnp.zeros((C,), jnp.float32), 'Wp': w(ks[8], C, C), 'bp': jnp.zeros((C,), jnp.float32)}
    _L0_xattn_all = _L0_xattn_setup()
    _L0_xattn_in = {k: v for k, v in _L0_xattn_all.items() if k in ('Wk', 'bk', 'Wq', 'bq', 'Wv', 'bv', 'Wck', 'bck', 'Wcq', 'bcq', 'Wcv', 'bcv', 'Wp', 'bp')}
    del _L0_xattn_all

    def _L0_ffn_setup():
        import jax, jax.numpy as jnp
        import numpy as np
        EMBED_DIM = 256
        MLP_RATIO = 4
        NUM_EXPERTS = 8
        CAPACITY = 1.0
        LN_EPS = 1e-05

        def _layernorm(y, gamma, beta):
            mu = jnp.mean(y, axis=-1, keepdims=True)
            var = jnp.mean(jnp.square(y - mu), axis=-1, keepdims=True)
            return (y - mu) * jax.lax.rsqrt(var + LN_EPS) * gamma + beta
        key = jax.random.key(seed)
        k0, k1, k2, k3, k4, k5 = jax.random.split(key, 6)
        d = EMBED_DIM
        dd = EMBED_DIM * MLP_RATIO
        n = NUM_EXPERTS
        x = jax.random.normal(k0, (4, 512, d), dtype=jnp.float32)
        gate_w = jax.random.normal(k1, (n, d), dtype=jnp.float32) * 0.02
        ln_gamma = jnp.ones((d,), dtype=jnp.float32)
        ln_beta = jnp.zeros((d,), dtype=jnp.float32)
        fc1s = jax.random.normal(k2, (n, dd, d), dtype=jnp.float32) * (1.0 / np.sqrt(d))
        b1s = jax.random.normal(k3, (n, dd), dtype=jnp.float32) * 0.02
        fc2s = jax.random.normal(k4, (n, d, dd), dtype=jnp.float32) * (1.0 / np.sqrt(dd))
        b2s = jax.random.normal(k5, (n, d), dtype=jnp.float32) * 0.02
        return {'x': x, 'gate_w': gate_w, 'ln_gamma': ln_gamma, 'ln_beta': ln_beta, 'fc1s': fc1s, 'b1s': b1s, 'fc2s': fc2s, 'b2s': b2s}
    _L0_ffn_all = _L0_ffn_setup()
    _L0_ffn_in = {k: v for k, v in _L0_ffn_all.items() if k in ('gate_w', 'ln_gamma', 'ln_beta', 'fc1s', 'b1s', 'fc2s', 'b2s')}
    del _L0_ffn_all
    return {'x': x, 'ctx_512': ctx_512, 'L0_xattn_Wk': _L0_xattn_in['Wk'], 'L0_xattn_bk': _L0_xattn_in['bk'], 'L0_xattn_Wq': _L0_xattn_in['Wq'], 'L0_xattn_bq': _L0_xattn_in['bq'], 'L0_xattn_Wv': _L0_xattn_in['Wv'], 'L0_xattn_bv': _L0_xattn_in['bv'], 'L0_xattn_Wck': _L0_xattn_in['Wck'], 'L0_xattn_bck': _L0_xattn_in['bck'], 'L0_xattn_Wcq': _L0_xattn_in['Wcq'], 'L0_xattn_bcq': _L0_xattn_in['bcq'], 'L0_xattn_Wcv': _L0_xattn_in['Wcv'], 'L0_xattn_bcv': _L0_xattn_in['bcv'], 'L0_xattn_Wp': _L0_xattn_in['Wp'], 'L0_xattn_bp': _L0_xattn_in['bp'], 'L0_ffn_gate_w': _L0_ffn_in['gate_w'], 'L0_ffn_ln_gamma': _L0_ffn_in['ln_gamma'], 'L0_ffn_ln_beta': _L0_ffn_in['ln_beta'], 'L0_ffn_fc1s': _L0_ffn_in['fc1s'], 'L0_ffn_b1s': _L0_ffn_in['b1s'], 'L0_ffn_fc2s': _L0_ffn_in['fc2s'], 'L0_ffn_b2s': _L0_ffn_in['b2s']}

def reference(x, ctx_512, L0_xattn_Wk, L0_xattn_bk, L0_xattn_Wq, L0_xattn_bq, L0_xattn_Wv, L0_xattn_bv, L0_xattn_Wck, L0_xattn_bck, L0_xattn_Wcq, L0_xattn_bcq, L0_xattn_Wcv, L0_xattn_bcv, L0_xattn_Wp, L0_xattn_bp, L0_ffn_gate_w, L0_ffn_ln_gamma, L0_ffn_ln_beta, L0_ffn_fc1s, L0_ffn_b1s, L0_ffn_fc2s, L0_ffn_b2s):
    import jax
    import jax.numpy as jnp

    def _L0_xattn_ref(x, cross_input, Wk, bk, Wq, bq, Wv, bv, Wck, bck, Wcq, bcq, Wcv, bcv, Wp, bp):
        import jax, jax.numpy as jnp
        import numpy as np
        B, T, TC, C, CC, H = (2, 512, 128, 256, 128, 16)
        D = C // H

        def _heads(t):
            b, l, _ = t.shape
            return t.reshape(b, l, H, D).transpose(0, 2, 1, 3)
        scale = np.float32(1.0 / np.sqrt(D))
        q = _heads(x @ Wq + bq)
        k = _heads(x @ Wk + bk)
        v = _heads(x @ Wv + bv)
        att = jnp.einsum('bhqd,bhkd->bhqk', q, k) * scale
        causal = jnp.tril(jnp.ones((T, T), bool))
        att = jnp.where(causal[None, None], att, -jnp.inf)
        y = jnp.einsum('bhqk,bhkd->bhqd', jax.nn.softmax(att, axis=-1), v)
        qc = _heads(x @ Wcq + bcq)
        kc = _heads(cross_input @ Wck + bck)
        vc = _heads(cross_input @ Wcv + bcv)
        attc = jnp.einsum('bhqd,bhkd->bhqk', qc, kc) * scale
        y = y + jnp.einsum('bhqk,bhkd->bhqd', jax.nn.softmax(attc, axis=-1), vc)
        y = y.transpose(0, 2, 1, 3).reshape(x.shape[0], T, C)
        return y @ Wp + bp

    def _L0_ffn_ref(x, gate_w, ln_gamma, ln_beta, fc1s, b1s, fc2s, b2s):
        import jax, jax.numpy as jnp
        import numpy as np
        EMBED_DIM = 256
        MLP_RATIO = 4
        NUM_EXPERTS = 8
        CAPACITY = 1.0
        LN_EPS = 1e-05

        def _layernorm(y, gamma, beta):
            mu = jnp.mean(y, axis=-1, keepdims=True)
            var = jnp.mean(jnp.square(y - mu), axis=-1, keepdims=True)
            return (y - mu) * jax.lax.rsqrt(var + LN_EPS) * gamma + beta
        og_shape = x.shape
        d = og_shape[-1]
        xf = x.reshape(-1, d)
        bs = xf.shape[0]
        n = gate_w.shape[0]
        k = int(bs * CAPACITY) // n
        scores = xf @ gate_w.T
        scores = (jnp.tanh(scores) + 1.0) * 0.5
        vals, idx = jax.lax.top_k(scores.T, k)
        kept_w = vals.T
        flat_idx = idx.T.reshape(-1)
        y = xf[flat_idx].reshape(k, n, d)
        y = _layernorm(y, ln_gamma, ln_beta)
        h = jnp.einsum('knd,nfd->knf', y, fc1s) + b1s
        h = jax.nn.gelu(h, approximate=True)
        o = jnp.einsum('knf,ndf->knd', h, fc2s) + b2s
        o = o * kept_w[:, :, None]
        out = xf.at[flat_idx].add(o.reshape(k * n, d))
        return out.reshape(og_shape)
    x = x + _L0_xattn_ref(_layernorm(x, axis=-1), ctx_512, L0_xattn_Wk, L0_xattn_bk, L0_xattn_Wq, L0_xattn_bq, L0_xattn_Wv, L0_xattn_bv, L0_xattn_Wck, L0_xattn_bck, L0_xattn_Wcq, L0_xattn_bcq, L0_xattn_Wcv, L0_xattn_bcv, L0_xattn_Wp, L0_xattn_bp)
    x = x + _L0_ffn_ref(_layernorm(x, axis=-1), L0_ffn_gate_w, L0_ffn_ln_gamma, L0_ffn_ln_beta, L0_ffn_fc1s, L0_ffn_b1s, L0_ffn_fc2s, L0_ffn_b2s)
    return x

_drawn_inputs = setup_inputs


def setup_inputs(seed=0):
    import zlib

    import numpy as np

    out = dict(_drawn_inputs(seed))
    spreads = {'L0_xattn_bk': (0.0, 0.8),
     'L0_xattn_bq': (0.0, 0.1),
     'L0_xattn_bv': (0.0, 0.1),
     'L0_xattn_bck': (0.0, 0.8),
     'L0_xattn_bcq': (0.0, 0.1),
     'L0_xattn_bcv': (0.0, 0.1),
     'L0_xattn_bp': (0.0, 0.1),
     'L0_ffn_ln_gamma': (1.0, 0.2),
     'L0_ffn_ln_beta': (0.0, 0.353)}
    factors = {'L0_ffn_b1s': 8.0, 'L0_ffn_b2s': 8.0}
    for name, (base, spread) in spreads.items():
        noise = np.random.default_rng([zlib.crc32(name.encode()), seed]).standard_normal(out[name].shape)
        drawn = base * np.exp(spread * noise) if base else spread * noise
        out[name] = jnp.asarray(drawn.astype(out[name].dtype))
    for name, factor in factors.items():
        out[name] = (out[name] * factor).astype(out[name].dtype)
    return out
```

```python
import itertools
from contextlib import ExitStack

import concourse.bass as bass
from concourse import mybir

F32 = mybir.dt.float32
BF16 = mybir.dt.bfloat16
I32 = mybir.dt.int32
U32 = mybir.dt.uint32
ALU = mybir.AluOpType
ACT = mybir.ActivationFunctionType
AX = mybir.AxisListType

P = 128
H, D = 16, 16
UH = 4
UNITS = H // UH
HALF_H = P // D
Q_PART = (0, 0, 1, 0, 2, 1)
K_PART = (0, 1, 0, 2, 0, 1)
ROWS = len(Q_PART) * D
SHIFT_ROWS = 2
KROWS = ROWS + SHIFT_ROWS
SCALE = float(D) ** -0.5
EPS = 1e-5
NEG = -1e30
TWO_ONES = 1.0 + 0x3f80 * 2.0 ** -23
CROSS_IT = 8
ITS = 12
A_PER_IT = 4
N_A = ITS * A_PER_IT
N_EXP = 2 * ITS


def pieces(first, last):
    at = {}
    for g in range(UNITS):
        if not (last and g == 3):
            at[g, 0] = "shift"
        if not (first and g == 0):
            at[g, 2] = "out_self"
        at[g, 10] = "out_cross"
    if not first:
        at.update({(0, 3): "v", (0, 4): "vc0", (0, 5): "vc1", (0, 6): "yT0", (0, 7): "yT1",
                   (1, 8): "proj0", (1, 9): "proj1", (2, 6): "zT0", (2, 7): "zT1", (2, 9): "gate"})
    if not last:
        at.update({(0, 8): "y0T0", (0, 9): "y0T1", (0, 11): "ctxT0", (1, 1): "ctxT1",
                   (1, 3): "q", (1, 4): "qc", (1, 5): "k", (1, 6): "kc0", (1, 7): "kc1",
                   (2, 3): "v", (2, 4): "vc0", (2, 5): "vc1",
                   (3, 3): "q", (3, 4): "qc", (3, 5): "k", (3, 6): "kc0", (3, 7): "kc1"})
    return dict(sorted(at.items()))


HALF_PIECES = ("q", "qc", "k", "kc0", "kc1")
V_PIECES = ("v", "vc0", "vc1")
PROLOGUE = (("gateT", 0), ("y0T0", 0), ("y0T1", 0), ("ctxT0", 0), ("ctxT1", 0), *((n, 0) for n in HALF_PIECES),
            *((n, 0) for n in V_PIECES), *((n, 1) for n in HALF_PIECES), *((n, 1) for n in V_PIECES))
EPILOGUE = ("out_self", "yT0", "yT1", "proj0", "proj1", "zT0", "zT1", "gate")
COL = {"q": (0, 512), "qc": (512, 1024), "k": (1024, 1536), "kc0": (1536, 2048), "kc1": (2048, 2560)}
BIAS = {"q": 0, "qc": 1, "k": 2, "kc0": 3, "kc1": 3}
Q_COLS, K_COLS = 1024, 1536


def half_of(name, g):
    if name in V_PIECES:
        return 1 if g == 0 else 0
    return 0 if g == 1 else 1


def piece_number(b, first, last, g, i):
    order = list(pieces(first, last))
    n = len(PROLOGUE) + 1 + order.index((g, i))
    if not first:
        n = n + len(pieces(True, False)) + (b - 1) * len(pieces(False, False))
    return n


class Unit:

    def __init__(self, b, g):
        self.b, self.g = b, g

    def __radd__(self, n):
        return n + UNITS * self.b + self.g

    __add__ = __radd__

    def __rmul__(self, n):
        return n * UNITS * self.b + n * self.g


def unit_parity(unit):
    return unit.g % 2


def unit_group(unit):
    return unit.g


def piece_args(name, b, g):
    if name == "shift":
        unit = Unit(b, g + 1) if g < UNITS - 1 else Unit(b + 1, 0)
    elif name == "out_self":
        unit = Unit(b, g - 1) if g else Unit(b - 1, UNITS - 1)
    else:
        unit = Unit(b, g)
    if name in ("yT0", "yT1", "proj0", "proj1", "zT0", "zT1", "gate"):
        return b - 1, 0, unit
    return b + 1, half_of(name, g), unit


def projection(name, b, g):
    if name not in COL:
        return None
    halves = 2 * b + 2 + half_of(name, g)
    return 10 * b + 10 + 5 * half_of(name, g) + HALF_PIECES.index(name), halves


def rest_place(name, hf):
    return (5 * hf + HALF_PIECES.index(name)) % 2


_CROSS = [("cross", h, t, c) for h in range(UH) for t in range(4) for c in range(2)]
_SELF = [("self", h, t, 0) for h in range(UH) for t in range(4)]
MAX_ORDER = [m for n in range(16) for m in (_CROSS[2 * n], _CROSS[2 * n + 1], _SELF[n])]


def attention(nc, x, ctx_in, w, z_rows, out, parts_dram, shift_dram, s_all):
    B, T, C = x.shape
    TC, CC = ctx_in.shape[1:]
    KT = C // P
    NT = T // P
    NC_T = TC // P
    E = w["gate_w"].shape[0]
    assert T == 512 and C == 2 * P and CC == P and NC_T == CROSS_IT and NT + CROSS_IT == ITS

    with ExitStack() as stack:
        def sb(name, shape, dt=F32):
            return stack.enter_context(nc.sbuf_tensor(name, shape, dt))

        def ps(name, shape):
            return stack.enter_context(nc.psum_tensor(name, shape, F32))

        def sem(name):
            return stack.enter_context(nc.semaphore(name))

        q_stack = sb("q_stack", [P, UNITS, UH, Q_COLS], BF16)
        k_stack = sb("k_stack", [P, UNITS, UH, K_COLS], BF16)
        probs = sb("probs", [P, 4, 2, T])
        parts = sb("parts", [P, 3, Q_COLS + K_COLS], BF16)
        rest = sb("rest", [P, 2, T])
        x_sb = sb("x_sb", [P, NT, C])
        c_sb = sb("c_sb", [P, NC_T, CC])
        y0T = sb("y0T", [P, KT, T])
        ctxT = sb("ctxT", [P, TC])
        v_self = sb("v_self", [P, 2, NT, HALF_H, 32])
        v_cross = sb("v_cross", [P, 2, NC_T, HALF_H, 32])
        w_q = sb("w_q", [P, KT, C]); w_k = sb("w_k", [P, KT, C]); w_v = sb("w_v", [P, KT, C])
        w_cq = sb("w_cq", [P, KT, C]); w_p = sb("w_p", [P, KT, C])
        w_ck = sb("w_ck", [P, C]); w_cv = sb("w_cv", [P, C])
        bias = sb("bias", [P, 4, 2])
        bias_v = sb("bias_v", [P, 3, KT])
        bias_p = sb("bias_p", [P, C])
        gate_n = sb("gate_n", [E, C])
        gateT = sb("gateT", [P, KT, E])
        u_sb = sb("u_sb", [P, 2, T])
        y_sb = sb("y_sb", [P, NT, C])
        y_add = sb("y_add", [P, NT, UH, D])
        rden = sb("rden", [P, 2, NT, UH])
        yT = sb("yT", [P, KT, T])
        x1 = sb("x1", [P, NT, C])
        z_sb = sb("z_sb", [P, NT, C + E])
        zT = sb("zT", [P, KT, T])
        th = sb("th", [P, NT, E])
        stats = sb("stats", [P, 2, NT, 6])
        mean_var = sb("mean_var", [P, 2, NT, 2])
        rstd = sb("rstd", [P, 2, NT])
        minus_half = sb("minus_half", [P, NT])
        ident = sb("ident", [P, P])
        ident_16 = sb("ident_16", [P, P], BF16)
        causal = sb("causal", [P, P], BF16)
        chunk_max = sb("chunk_max", [P, UH * NT, 2])
        row_max = sb("row_max", [P, 2, UH, 2, NT])
        pool_idle = sb("pool_idle", [P, 17])
        dve_idle = sb("dve_idle", [P, 1])
        shift = sb("shift", [2 * UH * NT, 2, P], BF16)

        score_ps = ps("score_ps", [P, 4, T])
        max_ps = ps("max_ps", [P, 2, T])
        out_ps = ps("out_ps", [P, T])
        piece_ps = ps("piece_ps", [P, T])

        weights_in = sem("weights_in")
        consts = sem("consts")
        gate_ready = sem("gate_ready")
        x_in = sem("x_in"); c_in = sem("c_in"); xr_in = sem("xr_in")
        stats_done = [sem("stats0_done"), sem("stats1_done")]
        mv_done = [sem("mv0_done"), sem("mv1_done")]
        rstd_step = [sem("rstd0_step"), sem("rstd1_step")]
        ln_done = [sem("ln0_done"), sem("ln1_done")]
        piece_full = sem("piece_full")
        piece_free = sem("piece_free")
        high_done = sem("high_done")
        mid_done = sem("mid_done")
        low_done = sem("low_done")
        parts_out = sem("parts_out")
        slot_in = [sem(f"slot_in{s}") for s in range(UNITS)]
        shift_high = sem("shift_high")
        maxin_ready = sem("maxin_ready")
        max_done = sem("max_done")
        rowmax_done = sem("rowmax_done")
        shift_out = sem("shift_out")
        shift_in = [sem(f"shift_in{s}") for s in range(UNITS)]
        scores_ready = sem("scores_ready")
        exp_done = sem("exp_done")
        mask_done = sem("mask_done")
        pv_done = sem("pv_done")
        u_ready = sem("u_ready")
        rden_done = sem("rden_done")
        y_part = sem("y_part"); y_done = sem("y_done")
        pool_set = sem("pool_set"); ones_set = sem("ones_set")
        xb_done = sem("xb_done")
        v_bias_done = sem("v_bias_done")
        tanh_done = sem("tanh_done"); expert_scores = sem("expert_scores")
        base_done = sem("base_done")
        z_out = sem("z_out"); base_out = sem("base_out")

        N_LOADS = 15

        END = piece_number(B - 1, False, True, 0, 0) + len(pieces(False, True))

        block = stack.enter_context(nc.Block())


        FILL = 16 * 2 * len(Q_PART)
        PARTS = 16 * len(HALF_PIECES)
        LOADS = 16 * N_LOADS

        def tokens(dram, n):
            return dram[n].rearrange("(t p) c -> p t c", p=P)

        @block.sync
        def _(sp):
            def load_inputs(n):
                sp.dma_start(x_sb[:], tokens(x, n)).then_inc(x_in, 16)
                sp.dma_start(c_sb[:], tokens(ctx_in, n)).then_inc(c_in, 16)

            def load_weights():
                for name, tile in (("Wq", w_q), ("Wcq", w_cq), ("Wk", w_k), ("Wv", w_v), ("Wp", w_p)):
                    sp.dma_start(tile[:], w[name].rearrange("(t p) c -> p t c", p=P)).then_inc(weights_in, 16)
                for name, tile in (("Wck", w_ck), ("Wcv", w_cv)):
                    sp.dma_start(tile[:], w[name]).then_inc(weights_in, 16)
                for n, name in enumerate(("bq", "bcq", "bk", "bck")):
                    sp.dma_start(bias[:, n, :], w[name].rearrange("(t p) -> p t", p=P),
                                 allow_slow_non_contiguous=True).then_inc(weights_in, 16)
                for n, name in enumerate(("bv", "bcv")):
                    sp.dma_start(bias_v[:, n, :], w[name].rearrange("(t p) -> p t", p=P),
                                 allow_slow_non_contiguous=True).then_inc(weights_in, 16)
                sp.dma_start(bias_p[:], w["bp"].rearrange("(o c) -> o c", o=1).broadcast_to([P, C]))\
                    .then_inc(weights_in, 16)
                sp.dma_start(gate_n[:], w["gate_w"]).then_inc(weights_in, 16)

            def store_parts(hf, name, number, stacked=None):
                a, e = COL[name]
                sp.wait_ge(low_done, number)
                if stacked is not None and name == HALF_PIECES[0]:
                    for slot in (2 * hf, 2 * hf + 1):
                        sp.wait_ge(slot_in[slot], stacked)
                sp.dma_start(parts_dram[hf, :, :, a:e].rearrange("t c n -> c t n"), parts[:, :, a:e])\
                    .then_inc(parts_out, 16)

            def fill(slot, halves):
                hf, at = slot // 2, slot % 2 * UH * D
                sp.wait_ge(parts_out, PARTS * halves)
                for r in range(len(Q_PART)):
                    rows = slice(D * r, D * r + D)
                    sp.dma_start(q_stack[rows, slot], parts_dram[hf, Q_PART[r], at:at + UH * D, 0:Q_COLS]
                                 .rearrange("(h d) n -> d h n", d=D)).then_inc(slot_in[slot], 16)
                    sp.dma_start(k_stack[rows, slot], parts_dram[hf, K_PART[r], at:at + UH * D, Q_COLS:]
                                 .rearrange("(h d) n -> d h n", d=D)).then_inc(slot_in[slot], 16)

            def put_shift(slot, number, piece):
                sp.wait_ge(piece_free, piece + 1)
                sp.dma_start(shift_dram[slot % 2].rearrange("t (r q) -> r t q", q=P), shift[:])\
                    .then_inc(shift_out, 16)
                sp.wait_ge(shift_out, 16 * number + 16)
                sp.dma_start(q_stack[ROWS:KROWS, slot].rearrange("p h n -> p (h n)"), shift_dram[slot % 2])\
                    .then_inc(shift_in[slot], 16)

            def store_results(n, done):
                sp.wait_ge(expert_scores, done)
                sp.dma_start(tokens(z_rows, n), z_sb[:]).then_inc(z_out, 16)
                sp.wait_ge(base_done, done)
                sp.dma_start(tokens(out, n), x1[:]).then_inc(base_out, 16)

            def stored(batches):
                sp.wait_ge(z_out, 16 * batches)
                sp.wait_ge(base_out, 16 * batches)

            def load_residual(n):
                sp.dma_start(x1[:], tokens(x, n)).then_inc(xr_in, 16)

            def batch(b, first, last):
                before, after = (b - 1, b + 1) if isinstance(b, int) else (sp.snap(b - 1), sp.snap(b + 1))
                for g in range(UNITS):
                    if g == 0 and not last:
                        sp.wait_ge(piece_free, piece_number(b, first, last, 0, 0))
                        load_inputs(after)
                    if g == 0 and first:
                        load_residual(b)
                    if not (last and g == 3):
                        put_shift((g + 1) % UNITS, 4 * b + g + 1, piece_number(b, first, last, g, 0))
                    if not last and g in (1, 3):
                        hf = g // 2
                        for n, name in enumerate(HALF_PIECES):
                            store_parts(hf, name, 10 * b + 10 + 5 * hf + n + 1, FILL * b + FILL)
                        sp.wait_ge(scores_ready, N_EXP * (4 * b + 2 * hf + 1))
                        fill(2 * hf, 2 * b + 3 + hf)
                    if not last and g in (2,):
                        sp.wait_ge(scores_ready, N_EXP * (4 * b + 2))
                        fill(1, 2 * b + 3)
                    if not first and g == 0:
                        sp.wait_ge(scores_ready, N_EXP * (4 * b))
                        fill(3, 2 * b + 2)
                    if not first and g == 2:
                        store_results(before, b)
                        stored(b)
                        load_residual(b)

            load_inputs(0)
            load_weights()
            for hf in range(2):
                for n, name in enumerate(HALF_PIECES):
                    store_parts(hf, name, 5 * hf + n + 1)
                fill(2 * hf, hf + 1)
                fill(2 * hf + 1, hf + 1)
            put_shift(0, 0, len(PROLOGUE))
            batch(0, True, False)
            with sp.Fori(1, B - 1) as b:
                batch(b, False, False)
            batch(B - 1, False, True)
            store_results(B - 1, B)
            stored(B)

        def score_span(i):
            if i < CROSS_IT:
                return 0, T, T + i * P
            return (i - CROSS_IT) * P, 0, (i - CROSS_IT) * P

        @block.tensor
        def _(pe):
            def score_pair(b, g, i, p):
                u = UNITS * b + g
                if not (isinstance(b, int) and u == 0 and i == 0):
                    pe.wait_ge(exp_done, N_EXP * u + 2 * i + p - 1)
                if i == 0 and p == 0:
                    pe.wait_ge(shift_in[g], 16 * b + 16)
                q0, qc, kc = score_span(i)
                for h in (2 * p, 2 * p + 1):
                    mm = pe.matmul(score_ps[:, h, q0:T], k_stack[0:KROWS, g, h, kc:kc + P],
                                   q_stack[0:KROWS, g, h, qc + q0:qc + T], start=True, stop=True)
                mm.then_inc(scores_ready, 1)

            def values(b, g, i, part):
                u = UNITS * b + g
                if part == 0 and i < CROSS_IT:
                    pe.wait_ge(exp_done, N_EXP * u + 2 * i + 2)
                elif part == 0:
                    pe.wait_ge(mask_done, 2 * NT * u + 2 * (i - CROSS_IT) + 2)
                if part == 0 and i in (0, CROSS_IT) and not (isinstance(b, int) and u == 0 and i == 0):
                    pe.wait_ge(u_ready, 2 * u + (i > 0))
                q0 = score_span(i)[0]
                v, kt = (v_cross, i) if i < CROSS_IT else (v_self, i - CROSS_IT)
                middle = T if kt == 0 else (q0 + T) // 2
                if part == 1 and kt == 0:
                    return
                cols = slice(middle, T) if part else slice(q0, middle)
                for h in range(UH):
                    mm = pe.matmul(out_ps[32 * h:32 * h + 32, cols], v[:, g // 2, kt, g % 2 * UH + h, :],
                                   probs[:, i % 2 * 2 + h // 2, h % 2, cols],
                                   start=kt == 0, stop=part == 1 and i in (CROSS_IT - 1, ITS - 1))
                if part == 1 or kt == 0:
                    mm.then_inc(pv_done, 1)

            def max_input(b, g, a):
                u = UNITS * b + g
                kind, h, qt, chunk = MAX_ORDER[a]
                if a == 0:
                    pe.wait_ge(slot_in[g], FILL * b + FILL)
                if not (isinstance(b, int) and u == 0 and a < 2):
                    pe.wait_ge(max_done, N_A * u + a - 1)
                if kind == "cross":
                    qc, k0, n = T + qt * P, T + chunk * T, T
                else:
                    qc, k0, n = qt * P, 0, (qt + 1) * P
                mm = pe.matmul(max_ps[:, a % 2, 0:n], q_stack[0:ROWS, g, h, qc:qc + P],
                               k_stack[0:ROWS, g, h, k0:k0 + n], start=True, stop=kind == "cross")
                if kind == "self":
                    mm = pe.matmul(max_ps[:, a % 2, n - P:n], ident_16[:], causal[:], start=False, stop=True)
                mm.then_inc(maxin_ready, 1)

            def transpose4(sources):
                for n, src in enumerate(sources):
                    mm = pe.transpose(piece_ps[:, n * P:(n + 1) * P], src, ident[:])
                return mm

            def product(dst, pairs):
                for n, (lhs, rhs) in enumerate(pairs):
                    mm = pe.matmul(dst, lhs, rhs, start=n == 0, stop=n == len(pairs) - 1)
                return mm

            def piece(name, n, b, hf, unit):
                if not (isinstance(n, int) and n == 0):
                    pe.wait_ge(piece_free, n)
                c = int(name[-1]) if name[-1].isdigit() else 0
                cols = slice(hf * P, hf * P + P)
                if name == "gateT":
                    for t in range(KT):
                        mm = pe.transpose(piece_ps[:, t * E:(t + 1) * E], gate_n[:, t * P:(t + 1) * P], ident[0:E, 0:E])
                elif name == "shift":
                    pe.wait_ge(rowmax_done, unit + 1)
                    mm = pe.transpose(piece_ps[0:2 * UH * NT, 0:P],
                                      row_max[:, unit_parity(unit)].rearrange("p h s t -> p (h s t)"), ident[:])
                elif name in ("out_cross", "out_self"):
                    s = int(name == "out_self")
                    pe.wait_ge(u_ready, 2 * unit + s + 1)
                    mm = transpose4([u_sb[:, s, t * P:(t + 1) * P] for t in range(NT)])
                elif name in ("yT0", "yT1"):
                    pe.wait_ge(y_done, UNITS * b + UNITS)
                    mm = transpose4([y_sb[:, t, c * P:(c + 1) * P] for t in range(NT)])
                elif name in ("proj0", "proj1"):
                    for t in (0, 1):
                        tok = slice((2 * c + t) * P, (2 * c + t + 1) * P)
                        mm = product(piece_ps[:, t * C:(t + 1) * C], [(yT[:, k, tok], w_p[:, k, :]) for k in range(KT)])
                elif name in ("zT0", "zT1"):
                    pe.wait_ge(ln_done[1], b + 1)
                    mm = transpose4([z_sb[:, t, c * P:(c + 1) * P] for t in range(NT)])
                elif name == "gate":
                    for t in range(NT):
                        mm = product(piece_ps[:, t * E:(t + 1) * E],
                                     [(zT[:, k, t * P:(t + 1) * P], gateT[:, k, :]) for k in range(KT)])
                elif name in ("y0T0", "y0T1"):
                    pe.wait_ge(ln_done[0], b + 1)
                    mm = transpose4([x_sb[:, t, c * P:(c + 1) * P] for t in range(NT)])
                elif name in ("ctxT0", "ctxT1"):
                    pe.wait_ge(c_in, 16 * b + 16)
                    mm = transpose4([c_sb[:, NT * c + t, :] for t in range(NT)])
                elif name in ("q", "qc", "k"):
                    wt = {"q": w_q, "qc": w_cq, "k": w_k}[name]
                    mm = product(piece_ps[:], [(wt[:, k, cols], y0T[:, k, :]) for k in range(KT)])
                elif name in ("kc0", "kc1"):
                    mm = product(piece_ps[:], [(w_ck[:, cols], ctxT[:, c * T:(c + 1) * T])])
                elif name == "v":
                    for t in range(NT):
                        mm = product(piece_ps[:, t * P:(t + 1) * P],
                                     [(y0T[:, k, t * P:(t + 1) * P], w_v[:, k, cols]) for k in range(KT)])
                elif name in ("vc0", "vc1"):
                    for t in range(NT):
                        tok = slice((NT * c + t) * P, (NT * c + t + 1) * P)
                        mm = product(piece_ps[:, t * P:(t + 1) * P], [(ctxT[:, tok], w_cv[:, cols])])
                mm.then_inc(piece_full, 1)

            def batch(b, first, last):
                at = pieces(first, last)
                for g in range(UNITS):
                    for i in range(ITS):
                        ahead = not (last and g >= 2)
                        to = (b, g + 2) if g < 2 else (b + 1, g - 2)
                        before = (b, g, i - 1) if i else (b, g - 1, ITS - 1) if g else (b - 1, UNITS - 1, ITS - 1)
                        for n in range(A_PER_IT):
                            if ahead:
                                max_input(*to, A_PER_IT * i + n)
                            if n < 2:
                                score_pair(b, g, i, n)
                            elif not (first and g == 0 and i == 0):
                                values(*before, n - 2)
                        if (g, i) in at:
                            piece(at[g, i], piece_number(b, first, last, g, i),
                                  *piece_args(at[g, i], b, g))

            pe.wait_ge(weights_in, LOADS)
            pe.wait_ge(consts, 3)
            for n, (name, hf) in enumerate(PROLOGUE):
                piece(name, n, 0, hf, 0)
            for a in range(N_A):
                max_input(0, 0, a)
            for a in range(N_A):
                max_input(0, 1, a)
            piece("shift", len(PROLOGUE), 0, 0, Unit(0, 0))
            pe.wait_ge(ones_set, 1)
            batch(0, True, False)
            with pe.Fori(1, B - 1) as b:
                batch(b, False, False)
            batch(B - 1, False, True)
            for part in range(2):
                values(B - 1, UNITS - 1, ITS - 1, part)
            for n, name in enumerate(EPILOGUE):
                piece(name, END + n, B - 1, 0, Unit(B - 1, UNITS - 1))

        @block.scalar
        def _(act):
            def exp_pair(b, g, i, p):
                u = UNITS * b + g
                q0 = score_span(i)[0]
                act.wait_ge(scores_ready, N_EXP * u + 2 * i + p + 1)
                if not (isinstance(b, int) and u == 0 and i < 2):
                    act.wait_ge(pv_done, ITS * u + i - 1)
                nc.scalar.activation(probs[:, i % 2 * 2 + p, :, q0:T], score_ps[:, 2 * p:2 * p + 2, q0:T],
                                     ACT.Exp, scale=SCALE).then_inc(exp_done, 1)

            def copy_out(b, g, s):
                u = UNITS * b + g
                act.wait_ge(pv_done, ITS * u + (ITS if s else CROSS_IT))
                if s == 0 and not (isinstance(b, int) and u == 0):
                    act.wait_ge(y_part, 2 * u - 1)
                elif s == 1:
                    act.wait_ge(y_part, 2 * u)
                nc.scalar.copy(u_sb[:, s, :], out_ps[:]).then_inc(u_ready, 1)

            def piece(name, n, b, hf, unit, k):
                c = int(name[-1]) if name[-1].isdigit() else 0
                if name in ("out_cross", "out_self", "proj0", "proj1"):
                    return
                act.wait_ge(piece_full, n + 1)
                if name == "gateT":
                    nc.scalar.copy(gateT[:].rearrange("p t e -> p (t e)"), piece_ps[:, 0:KT * E]).then_inc(piece_free, 1)
                elif name == "shift":
                    act.wait_ge(shift_out, 16 * unit)
                    nc.scalar.mul(shift[:, 0, :], piece_ps[0:2 * UH * NT, 0:P], -1.0).then_inc(shift_high, 1)
                elif name in ("yT0", "yT1"):
                    nc.scalar.activation(yT[:, c, :], piece_ps[:], ACT.Identity, bias=bias_v[:, 2, c:c + 1])\
                        .then_inc(piece_free, 1)
                elif name in ("zT0", "zT1", "y0T0", "y0T1"):
                    dst = (y0T if name[0] == "y" else zT)[:, c, :]
                    nc.scalar.copy(dst, piece_ps[:]).then_inc(piece_free, 1)
                elif name in ("ctxT0", "ctxT1"):
                    nc.scalar.copy(ctxT[:, c * T:(c + 1) * T], piece_ps[:]).then_inc(piece_free, 1)
                elif name == "gate":
                    nc.scalar.activation(th[:].rearrange("p t e -> p (t e)"), piece_ps[:, 0:NT * E], ACT.Tanh)\
                        .then_inc(piece_free, 1)
                elif name in COL:
                    a, e = COL[name]
                    halves = k[1]
                    if not (isinstance(halves, int) and halves == 0):
                        act.wait_ge(parts_out, PARTS * halves)
                    nc.scalar.activation(parts[:, 0, a:e], piece_ps[:], ACT.Identity,
                                         bias=bias[:, BIAS[name], hf:hf + 1]).then_inc(high_done, 1)
                else:
                    v = (v_self if name == "v" else v_cross)[:, hf, NT * c:NT * c + NT, :, 0:D]
                    nc.scalar.copy(v, piece_ps[:].rearrange("p (t h d) -> p t h d", t=NT, d=D)).then_inc(piece_free, 1)

            def batch(b, first, last):
                at = pieces(first, last)
                for g in range(UNITS):
                    for i in range(ITS):
                        exp_pair(b, g, i, 0)
                        gi = (g, i - 1) if i else (g - 1, ITS - 1)
                        if gi in at:
                            piece(at[gi], piece_number(b, first, last, *gi),
                                  *piece_args(at[gi], b, gi[0]), projection(at[gi], b, gi[0]))
                        exp_pair(b, g, i, 1)
                        if i == 0 and g > 0:
                            copy_out(b, g - 1, 1)
                        elif i == 0 and not first:
                            copy_out(b - 1, UNITS - 1, 1)
                        elif i == CROSS_IT:
                            copy_out(b, g, 0)

            act.wait_ge(weights_in, LOADS)
            act.wait_ge(consts, 3)
            act.wait_ge(v_bias_done, 1)
            for n, (name, hf) in enumerate(PROLOGUE):
                piece(name, n, 0, hf, 0, (0, hf))
            piece("shift", len(PROLOGUE), 0, 0, Unit(0, 0), None)
            batch(0, True, False)
            with act.Fori(1, B - 1) as b:
                batch(b, False, False)
            batch(B - 1, False, True)
            copy_out(B - 1, UNITS - 1, 1)
            for n, name in enumerate(EPILOGUE):
                piece(name, END + n, B - 1, 0, Unit(B - 1, UNITS - 1), None)

        @block.vector
        def _(dve):
            def maximum(b, g, a):
                u = UNITS * b + g
                kind, h, qt, chunk = MAX_ORDER[a]
                bank = max_ps[:, a % 2]
                if a == 0 and not (isinstance(u, int) and u == 0):
                    dve.wait_ge(rowmax_done, u)
                n = T if kind == "cross" else (qt + 1) * P
                dst = (chunk_max[:, h * NT + qt, chunk:chunk + 1] if kind == "cross"
                       else row_max[:, g % 2, h, 0, qt:qt + 1])
                dve.wait_ge(maxin_ready, N_A * u + a + 1)
                nc.vector.tensor_reduce(dst, bank[:, 0:n], AX.X, ALU.max).then_inc(max_done, 1)

            def finish_maxima(b, g):
                u = UNITS * b + g
                dve.wait_ge(max_done, N_A * u + N_A)
                nc.vector.tensor_reduce(row_max[:, g % 2, :, 1, :], chunk_max[:].rearrange("p (h t) c -> p h t c", h=UH),
                                        AX.X, ALU.max).then_inc(rowmax_done, 1)

            def norm_stats(which, rows, count):
                for t in range(NT):
                    st = nc.vector.bn_stats(stats[:, which, t, :], rows(t))
                st.then_inc(stats_done[which], 1)
                dve.wait_ge(stats_done[which], count)
                nc.vector.memset(dve_idle[:], 0.0)
                for t in range(NT):
                    ag = nc.vector.bn_aggr(mean_var[:, which, t, :], stats[:, which, t, :])
                ag.then_inc(mv_done[which], 1)

            def piece(name, n, b, hf, unit, k):
                if name == "shift":
                    dve.wait_ge(shift_high, unit + 1)
                    nc.vector.scalar_tensor_tensor(
                        out=shift[:, 1, :], in0=piece_ps[0:2 * UH * NT, 0:P], scalar=-1.0, in1=shift[:, 0, :],
                        op0=ALU.mult, op1=ALU.subtract).then_inc(piece_free, 1)
                elif name in ("out_cross", "out_self"):
                    s = int(name == "out_self")
                    g = unit_group(unit)
                    sums = piece_ps[:].rearrange("p (t h d) -> p t h d", t=NT, h=UH)
                    dve.wait_ge(piece_full, n + 1)
                    nc.vector.reciprocal(rden[:, s], sums[:, :, :, D]).then_inc(rden_done, 1)
                    if s:
                        dve.wait_ge(y_done, unit + 0)
                        y = y_add[:]
                    else:
                        y = y_sb[:, :, g * UH * D:(g + 1) * UH * D].rearrange("p t (h d) -> p t h d", h=UH)
                    dve.wait_ge(rden_done, 2 * unit + s + 1)
                    nc.vector.tensor_tensor(y, sums[:, :, :, 0:D], rden[:, s].unsqueeze(3).broadcast_to([P, NT, UH, D]),
                                            ALU.mult).then_inc(y_part, 1)
                    dve.wait_ge(y_part, 2 * unit + s + 1)
                    nc.vector.memset(dve_idle[:], 0.0).then_inc(piece_free, 1)
                elif name in ("proj0", "proj1"):
                    c = int(name[-1])
                    dve.wait_ge(xb_done, b + 1)
                    dve.wait_ge(piece_full, n + 1)
                    rows = x1[:, 2 * c:2 * c + 2, :].rearrange("p t c -> p (t c)")
                    nc.vector.tensor_tensor(rows, piece_ps[:], rows, ALU.add).then_inc(piece_free, 1)
                    if c == 1:
                        dve.wait_ge(piece_free, n + 1)
                        norm_stats(1, lambda t: x1[:, t, :], b + 1)
                elif name == "gate":
                    dve.wait_ge(piece_free, n + 1)
                    nc.vector.tensor_scalar(s_all[:, :, bass.ds(b * NT, NT)], th[:].rearrange("p t e -> p e t"),
                                            1.0, 0.5, ALU.add, ALU.mult)
                    nc.vector.tensor_scalar(z_sb[:, :, C:C + E], th[:], 1.0, 0.5, ALU.add, ALU.mult)\
                        .then_inc(expert_scores, 1)
                elif name in COL:
                    a, e = COL[name]
                    dve.wait_ge(high_done, k[0] + 1)
                    if not (isinstance(k[0], int) and k[0] < 2):
                        dve.wait_ge(low_done, k[0] - 1)
                    nc.vector.scalar_tensor_tensor(
                        out=rest[:, rest_place(name, hf)], in0=piece_ps[:], scalar=bias[:, BIAS[name], hf:hf + 1],
                        in1=parts[:, 0, a:e], op0=ALU.add, op1=ALU.subtract).then_inc(piece_free, 1)

            def batch(b, first, last):
                at = pieces(first, last)
                for g in range(UNITS):
                    ahead = not (last and g >= 2)
                    to = (b, g + 2) if g < 2 else (b + 1, g - 2)
                    for i in range(ITS):
                        if ahead:
                            maximum(*to, A_PER_IT * i)
                        gi = (g, i - 1) if i else (g - 1, ITS - 1)
                        if gi in at:
                            piece(at[gi], piece_number(b, first, last, *gi),
                                  *piece_args(at[gi], b, gi[0]), projection(at[gi], b, gi[0]))
                        if ahead:
                            for a in (1, 2, 3):
                                maximum(*to, A_PER_IT * i + a)
                        if (g, i) == (0, 4) and not last:
                            dve.wait_ge(x_in, 16 * b + 32)
                            norm_stats(0, lambda t: x_sb[:, t, :], b + 2)
                    if ahead:
                        finish_maxima(*to)

            dve.wait_ge(x_in, 16)
            norm_stats(0, lambda t: x_sb[:, t, :], 1)
            nc.vector.memset(k_stack[ROWS:KROWS].rearrange("p s h n -> p (s h n)").bitcast(F32), TWO_ONES)\
                .then_inc(ones_set, 1)
            dve.wait_ge(weights_in, LOADS)
            nc.vector.tensor_tensor(bias_v[:, 2, :], bias_v[:, 0, :], bias_v[:, 1, :], ALU.add).then_inc(v_bias_done, 1)
            for n, (name, hf) in enumerate(PROLOGUE):
                piece(name, n, 0, hf, 0, (5 * hf + [*HALF_PIECES, name].index(name), hf))
            for v in range(2):
                for a in range(N_A):
                    maximum(0, v, a)
                finish_maxima(0, v)
            piece("shift", len(PROLOGUE), 0, 0, Unit(0, 0), None)
            batch(0, True, False)
            with dve.Fori(1, B - 1) as b:
                batch(b, False, False)
            batch(B - 1, False, True)
            for n, name in enumerate(EPILOGUE):
                piece(name, END + n, B - 1, 0, Unit(B - 1, UNITS - 1), None)

        @block.gpsimd
        def _(pool):
            idle = itertools.cycle(range(1, 17))

            def hold():
                c = next(idle)
                nc.gpsimd.tensor_tensor(pool_idle[:, c:c + 1], pool_idle[:, 0:1], pool_idle[:, 0:1], ALU.add)

            def normalize(which, dst, src, count):
                pool.wait_ge(mv_done[which], count)
                hold()
                nc.gpsimd.tensor_scalar(rstd[:, which], mean_var[:, which, :, 1], EPS, None, ALU.add)\
                    .then_inc(rstd_step[which], 1)
                pool.wait_ge(rstd_step[which], 2 * count - 1)
                nc.gpsimd.tensor_tensor(rstd[:, which], rstd[:, which], minus_half[:], ALU.pow)\
                    .then_inc(rstd_step[which], 1)
                pool.wait_ge(rstd_step[which], 2 * count)
                hold()
                for t in range(NT):
                    nz = nc.gpsimd.tensor_scalar(dst(t), src(t), mean_var[:, which, t, 0:1], rstd[:, which, t:t + 1],
                                                 ALU.subtract, ALU.mult)
                nz.then_inc(ln_done[which], 1)

            def split(name, n, hf, k):
                a, e = COL[name]
                src = rest[:, rest_place(name, hf)]
                pool.wait_ge(piece_free, n + 1)
                hold()
                nc.gpsimd.tensor_copy(parts[:, 1, a:e], src).then_inc(mid_done, 1)
                pool.wait_ge(mid_done, k + 1)
                nc.gpsimd.tensor_tensor(parts[:, 2, a:e], src, parts[:, 1, a:e], ALU.subtract).then_inc(low_done, 1)

            def residual(n):
                pool.wait_ge(xr_in, 16 * n + 16)
                for t in range(NT):
                    xb = nc.gpsimd.tensor_tensor(x1[:, t, :], x1[:, t, :], bias_p[:], ALU.add)
                xb.then_inc(xb_done, 1)

            def second_norm(n):
                normalize(1, lambda t: z_sb[:, t, 0:C], lambda t: x1[:, t, :], n + 1)
                pool.wait_ge(ln_done[1], n + 1)
                nc.gpsimd.tensor_tensor(x1[:], x1[:], z_sb[:, :, 0:C], ALU.add).then_inc(base_done, 1)

            def add_heads(n, unit):
                g = unit_group(unit)
                y = y_sb[:, :, g * UH * D:(g + 1) * UH * D]
                pool.wait_ge(piece_free, n + 1)
                nc.gpsimd.tensor_tensor(y, y, y_add[:].rearrange("p t h d -> p t (h d)"), ALU.add).then_inc(y_done, 1)

            def mask(b, g, i):
                q0 = score_span(i)[0]
                for p in range(2):
                    pool.wait_ge(exp_done, N_EXP * (UNITS * b + g) + 2 * i + p + 1)
                    hold()
                    tile = probs[:, i % 2 * 2 + p, :, q0:q0 + P]
                    nc.gpsimd.affine_select(out=tile, in_=tile, pattern=[[0, 2], [1, P]], compare_op=ALU.is_ge,
                                            fill=0.0, base=0, channel_multiplier=-1).then_inc(mask_done, 1)

            def batch(b, first, last):
                at = pieces(first, last)
                for g in range(UNITS):
                    if (g, 0) == (2, 0) and not first:
                        second_norm(b - 1)
                    for i in range(ITS):
                        if i >= CROSS_IT:
                            mask(b, g, i)
                        gi = (g, i - 1) if i else (g - 1, ITS - 1)
                        if gi in at:
                            name, n = at[gi], piece_number(b, first, last, *gi)
                            if name == "out_self":
                                add_heads(n, piece_args(name, b, gi[0])[2])
                            elif name in COL:
                                split(name, n, piece_args(name, b, gi[0])[1], projection(name, b, gi[0])[0])
                        if (g, i) == (0, 5) and not last:
                            normalize(0, lambda t: x_sb[:, t, :], lambda t: x_sb[:, t, :], b + 2)
                        if (g, i) == (0, 6) and not first:
                            residual(b - 1)

            nc.gpsimd.memset(ident[:], 0.0)
            nc.gpsimd.memset(causal[:], 0.0)
            nc.gpsimd.memset(minus_half[:], -0.5)
            nc.gpsimd.memset(pool_idle[:], 0.0).then_inc(pool_set, 1)
            pool.wait_ge(pool_set, 1)
            nc.gpsimd.affine_select(out=ident[:], in_=ident[:], compare_op=ALU.not_equal, fill=1.0, base=0,
                                    pattern=[[-1, P]], channel_multiplier=1).then_inc(consts, 1)
            nc.gpsimd.affine_select(out=ident_16[:], in_=causal[:], compare_op=ALU.not_equal, fill=1.0, base=0,
                                    pattern=[[-1, P]], channel_multiplier=1).then_inc(consts, 1)
            nc.gpsimd.memset(v_self[:], 1.0)
            nc.gpsimd.memset(v_cross[:], 1.0)
            pool.wait_ge(consts, 2)
            nc.gpsimd.affine_select(out=causal[:], in_=causal[:], compare_op=ALU.is_ge, fill=NEG,
                                    base=0, pattern=[[-1, P]], channel_multiplier=1).then_inc(consts, 1)
            normalize(0, lambda t: x_sb[:, t, :], lambda t: x_sb[:, t, :], 1)
            for n, (name, hf) in enumerate(PROLOGUE):
                if name in COL:
                    split(name, n, hf, 5 * hf + HALF_PIECES.index(name))
            batch(0, True, False)
            with pool.Fori(1, B - 1) as b:
                batch(b, False, False)
            batch(B - 1, False, True)
            add_heads(END, Unit(B - 1, UNITS - 1))
            residual(B - 1)
            second_norm(B - 1)


FF_PROLOGUE_ITEMS = 7
FF_ITEMS = 14


def feed_forward(nc, w, z_rows, out, s_all):
    E, F, C = w["fc1s"].shape
    NTOK = z_rows.shape[0] * z_rows.shape[1]
    W_ROW = z_rows.shape[2]
    K = NTOK // E
    TILES = NTOK // P
    KT, FT, NT = C // P, F // P, K // P
    assert C == 2 * P and K == 512
    ROUNDS = 26
    z_flat = z_rows.rearrange("b t c -> (b t) c")
    out_flat = out.rearrange("b t c -> (b t) c")

    with ExitStack() as stack:
        def sb(name, shape, dt=F32):
            return stack.enter_context(nc.sbuf_tensor(name, shape, dt))

        def ps(name, shape):
            return stack.enter_context(nc.psum_tensor(name, shape, F32))

        def sem(name):
            return stack.enter_context(nc.semaphore(name))

        w1_n = sb("w1_n", [P, FT, C]); w2_n = sb("w2_n", [P, KT, F])
        w1T = sb("w1T", [P, KT, F]); w2T = sb("w2T", [P, FT, C])
        b1_n = sb("b1_n", [E * FT, P]); b1T = sb("b1T", [P, E * FT])
        b2 = sb("b2", [P, C])
        gamma = sb("gamma", [P, KT]); beta = sb("beta", [P, KT])
        rows = sb("rows", [P, NT, W_ROW])
        y = sb("y", [P, NT, C])
        yT = sb("ff_yT", [P, KT, K])
        h = sb("h", [P, FT, K])
        o = sb("o", [P, NT, C])
        weight = sb("weight", [P, NT])
        stats = sb("ff_stats", [P, NT, 6]); mean_var = sb("ff_mv", [P, NT, 2]); rstd = sb("ff_rstd", [P, NT])
        minus_half = sb("ff_minus_half", [P, NT])
        pool_idle = sb("ff_pool_idle", [P, 17]); dve_idle = sb("ff_dve_idle", [P, 1])
        ident = sb("ff_ident", [P, P])
        ones = sb("ones", [P, P], BF16); upto = sb("upto", [P, P], BF16)
        iota = sb("iota", [P, P], BF16)
        token = sb("token", [P, 2, TILES], BF16)
        low = sb("low", [P, E]); high = sb("high", [P, E]); both = sb("both", [P, E]); mid = sb("mid", [P, E])
        low_try = sb("low_try", [P, E]); high_try = sb("high_try", [P, E]); count = sb("count", [P, E])
        above = sb("above", [P, E, TILES], BF16); tied = sb("tied", [P, E, TILES], BF16)
        chosen = sb("chosen", [P, E, TILES], BF16)
        not_first = sb("not_first", [P, E, TILES]); scan = sb("scan", [P, E, TILES])
        place = sb("place", [P, E, TILES]); tmp = sb("tmp", [P, E, TILES])
        room = sb("room", [P, E]); thr = sb("thr", [P, E])
        e_place = sb("e_place", [P, TILES]); e_col = sb("e_col", [P, 4, TILES]); e_row = sb("e_row", [P, TILES])
        onehot = sb("onehot", [P, 4, P], BF16)
        e_rhs = sb("e_rhs", [P, TILES, 2, NT], BF16)
        e_list = sb("e_list", [P, 2 * NT])
        index_next = sb("index_next", [P, NT], I32); index = sb("index", [P, NT], I32)

        h_ps = ps("h_ps", [P, 2, K])
        o_ps = ps("o_ps", [P, 2, 512])
        transpose_ps = ps("transpose_ps", [P, 2, 512])
        count_ps = ps("count_ps", [P, 2, E * TILES])
        list_ps = ps("list_ps", [P, 512])

        w1_in = sem("w1_in"); w2_in = sem("w2_in"); b2_in = sem("b2_in"); small_in = sem("small_in")
        consts = sem("ff_consts"); pool_set = sem("ff_pool_set")
        tested = sem("tested"); counted = sem("counted"); round_step = sem("round_step")
        route = sem("route"); route_ps = sem("route_ps")
        item_full = sem("item_full"); item_free = sem("item_free")
        list_step = sem("list_step"); onehot_ready = sem("onehot_ready"); onehot_used = sem("onehot_used")
        list_full = sem("list_full"); index_ready = sem("index_ready")
        rows_in = sem("rows_in"); stats_done = sem("ff_stats_done"); mv_done = sem("ff_mv_done")
        rstd_step = sem("ff_rstd_step"); y_done = sem("ff_y_done")
        expert_set = sem("expert_set"); weight_set = sem("weight_set")
        h_full = sem("h_full"); h_done = sem("h_done")
        o_full = sem("o_full"); o_biased = sem("o_biased"); o_done = sem("o_done")
        added = sem("added")

        block = stack.enter_context(nc.Block())

        @block.sync
        def _(sp):
            def load_w1(e):
                sp.dma_start(w1_n[:], w["fc1s"][e].rearrange("(t p) c -> p t c", p=P)).then_inc(w1_in, 16)

            def load_w2(e):
                sp.dma_start(w2_n[:], w["fc2s"][e].rearrange("(t p) f -> p t f", p=P)).then_inc(w2_in, 16)

            def load_b2(e):
                sp.dma_start(b2[:], w["b2s"][bass.ds(e, 1), :].broadcast_to([P, C])).then_inc(b2_in, 16)

            def expert(e, last):
                nxt = e + 1 if isinstance(e, int) else sp.snap(e + 1)
                if not last:
                    sp.wait_ge(item_free, FF_PROLOGUE_ITEMS - KT + FF_ITEMS * e)
                    load_w1(nxt)
                    sp.wait_ge(item_free, FF_PROLOGUE_ITEMS + FF_ITEMS * e + FT)
                    load_w2(nxt)
                    sp.wait_ge(o_biased, NT * e + NT)
                    load_b2(nxt)

            load_w1(0)
            load_w2(0)
            load_b2(0)
            sp.dma_start(b1_n[:], w["b1s"].rearrange("e (t p) -> (e t) p", p=P)).then_inc(small_in, 16)
            for name, tile in (("ln_gamma", gamma), ("ln_beta", beta)):
                sp.dma_start(tile[:], w[name].rearrange("(t p) -> p t", p=P),
                             allow_slow_non_contiguous=True).then_inc(small_in, 16)
            with sp.Fori(0, E - 1) as e:
                expert(e, False)

        @block.tensor
        def _(pe):
            def item(n, j, pairs):
                if not (isinstance(n, int) and n < 2):
                    pe.wait_ge(item_free, n - 1)
                bank = j % 2
                for (a, src) in pairs:
                    k = src.shape[0]
                    mm = pe.transpose(transpose_ps[:, bank, a:a + k], src, ident[0:k, 0:k])
                mm.then_inc(item_full, 1)

            def item_w1(n, j, e, t):
                if t == 0:
                    pe.wait_ge(w1_in, 16 * e + 16)
                item(n, j, [((2 * k + f) * P, w1_n[:, 2 * t + f, k * P:(k + 1) * P])
                               for k in range(KT) for f in range(2)])

            def item_w2(n, j, e, f):
                if f == 0:
                    pe.wait_ge(w2_in, 16 * e + 16)
                item(n, j, [(k * P, w2_n[:, k, f * P:(f + 1) * P]) for k in range(KT)])

            def item_y(n, j, e, k):
                pe.wait_ge(y_done, e + 1)
                item(n, j, [(t * P, y[:, t, k * P:(k + 1) * P]) for t in range(NT)])

            def list_products(e):
                for t in range(TILES):
                    pe.wait_ge(onehot_ready, TILES * e + t + 1)
                    mm = pe.matmul(list_ps[:, 0:2 * NT], onehot[:, t % 4], e_rhs[:, t].rearrange("p v c -> p (v c)"),
                                   start=t == 0, stop=t == TILES - 1)
                    mm.then_inc(onehot_used, 1)

            def expert(e, last):
                n0 = FF_PROLOGUE_ITEMS + FF_ITEMS * e
                for f in range(FT):
                    if f == 0:
                        pe.wait_ge(item_free, n0)
                    if f >= 2:
                        pe.wait_ge(h_done, FT * e + f - 1)
                    for k in range(KT):
                        mm = pe.matmul(h_ps[:, f % 2], w1T[:, k, f * P:(f + 1) * P], yT[:, k, :],
                                       start=k == 0, stop=k == KT - 1)
                    mm.then_inc(h_full, 1)
                    item_w2(n0 + f, f + 1, e, f)
                if not last:
                    list_products(e + 1)
                pe.wait_ge(item_free, n0 + FT)
                pe.wait_ge(h_done, FT * e + FT)
                for t in range(NT):
                    if t >= 2:
                        pe.wait_ge(o_biased, NT * e + t - 1)
                    for f in range(FT):
                        mm = pe.matmul(o_ps[:, t % 2, 0:C], h[:, f, t * P:(t + 1) * P], w2T[:, f, :],
                                       start=f == 0, stop=f == FT - 1)
                    mm.then_inc(o_full, 1)
                    if not last:
                        item_w1(n0 + FT + t, FT + t + 1, e + 1, t)
                if not last:
                    for k in range(KT):
                        item_y(n0 + FT + NT + k, FT + NT + k + 1, e + 1, k)

            pe.wait_ge(consts, 3)
            with pe.Fori(0, ROUNDS) as r:
                pe.wait_ge(tested, r + 1)
                pe.matmul(count_ps[:, 0, :], ones[:], chosen[:].rearrange("p e t -> p (e t)"),
                          start=True, stop=True).then_inc(counted, 1)
            pe.wait_ge(route, 2)
            pe.matmul(count_ps[:, 0, :], ones[:], above[:].rearrange("p e t -> p (e t)"), start=True, stop=True)\
                .then_inc(route_ps, 1)
            pe.wait_ge(route, 4)
            for n, tile in enumerate((tied, chosen)):
                flat = tile[:].rearrange("p e t -> p (e t)")
                if n:
                    pe.wait_ge(route, CHOSEN_STEP)
                pe.matmul(count_ps[:, 0, :], upto[:], flat, start=True, stop=True)
                pe.matmul(count_ps[:, 1, :], ones[:], flat, start=True, stop=True).then_inc(route_ps, 1)
            pe.wait_ge(small_in, 48)
            item(0, 0, [(0, b1_n[:])])
            for t in range(NT):
                item_w1(1 + t, 1 + t, 0, t)
            list_products(0)
            for k in range(KT):
                item_y(1 + NT + k, 1 + NT + k, 0, k)
            with pe.Fori(0, E - 1) as e:
                expert(e, False)
            expert(E - 1, True)

        @block.scalar
        def _(act):
            def expert(e):
                for f in range(FT):
                    act.wait_ge(h_full, FT * e + f + 1)
                    nc.scalar.activation(h[:, f, :], h_ps[:, f % 2], ACT.Gelu_apprx_tanh, bias=b1T[:, bass.ds(e * FT + f, 1)])\
                        .then_inc(h_done, 1)

            act.preload_act_table(ACT.Gelu_apprx_tanh)
            act.wait_ge(item_free, 1)
            with act.Fori(0, E) as e:
                expert(e)

        @block.vector
        def _(dve):
            def free_item(n, e, dst, src, scale=None):
                dve.wait_ge(item_full, n + 1)
                if scale is None:
                    nc.vector.tensor_copy(dst, src).then_inc(item_free, 1)
                else:
                    nc.vector.tensor_scalar(dst, src, *scale, ALU.mult, ALU.add).then_inc(item_free, 1)

            def item_w1(n, j, e, t):
                src = transpose_ps[:, j % 2].rearrange("p (k f) -> p k f", k=KT)
                free_item(n, e, w1T[:, :, 2 * t * P:(2 * t + 2) * P], src)

            def item_w2(n, j, e, f):
                free_item(n, e, w2T[:, f, :], transpose_ps[:, j % 2, 0:C])

            def item_y(n, j, e, k):
                free_item(n, e, yT[:, k, :], transpose_ps[:, j % 2], (gamma[:, k:k + 1], beta[:, k:k + 1]))

            def make_list(e):
                s = LIST_STEPS * e
                if not (isinstance(e, int) and e == 0):
                    dve.wait_ge(list_full, 2 * e)
                nc.vector.tensor_copy(e_place[:], place[:, bass.ds(e, 1), :].rearrange("p o t -> p (o t)"))\
                    .then_inc(list_step, 1)
                dve.wait_ge(list_step, s + 1)
                for c in range(1, NT):
                    st = nc.vector.tensor_scalar(e_col[:, c, :], e_place[:], c * P - 0.5, None, ALU.is_ge)
                st.then_inc(list_step, 1)
                dve.wait_ge(list_step, s + 2)
                nc.vector.tensor_scalar(e_col[:, 0, :], e_place[:], -0.5, None, ALU.is_ge)
                nc.vector.scalar_tensor_tensor(out=e_row[:], in0=e_col[:, 1, :], scalar=-float(P), in1=e_place[:],
                                               op0=ALU.mult, op1=ALU.add).then_inc(list_step, 1)
                for c in range(2, NT):
                    dve.wait_ge(list_step, s + c + 1)
                    nc.vector.scalar_tensor_tensor(out=e_row[:], in0=e_col[:, c, :], scalar=-float(P), in1=e_row[:],
                                                   op0=ALU.mult, op1=ALU.add).then_inc(list_step, 1)
                dve.wait_ge(list_step, s + NT + 1)
                for c in range(NT - 1):
                    st = nc.vector.tensor_tensor(e_col[:, c, :], e_col[:, c, :], e_col[:, c + 1, :], ALU.subtract)\
                        .then_inc(list_step, 1)
                    dve.wait_ge(list_step, s + NT + 2 + c)
                for v in range(2):
                    for c in range(NT):
                        st = nc.vector.tensor_tensor(e_rhs[:, :, v, c], e_col[:, c, :], token[:, v, :], ALU.mult)
                st.then_inc(list_step, 1)
                dve.wait_ge(list_step, s + 2 * NT + 1)
                for t in range(TILES):
                    if not (isinstance(e, int) and e == 0 and t < 4):
                        dve.wait_ge(onehot_used, TILES * e + t - 3)
                    nc.vector.tensor_scalar(onehot[:, t % 4], iota[:], e_row[:, t:t + 1], None, ALU.is_equal)\
                        .then_inc(onehot_ready, 1)
                dve.wait_ge(onehot_used, TILES * e + TILES)
                nc.vector.tensor_copy(e_list[:], list_ps[:, 0:2 * NT]).then_inc(list_full, 1)
                dve.wait_ge(list_full, 2 * e + 1)
                if not (isinstance(e, int) and e == 0):
                    dve.wait_ge(expert_set, e)
                nc.vector.scalar_tensor_tensor(out=index_next[:], in0=e_list[:, 0:NT], scalar=float(P),
                                               in1=e_list[:, NT:2 * NT], op0=ALU.mult, op1=ALU.add)\
                    .then_inc(list_full, 1)

            def norm_stats(e):
                dve.wait_ge(rows_in, 16 * NT * (e + 1))
                for t in range(NT):
                    st = nc.vector.bn_stats(stats[:, t, :], rows[:, t, 0:C])
                st.then_inc(stats_done, 1)
                dve.wait_ge(stats_done, e + 1)
                nc.vector.memset(dve_idle[:], 0.0)
                for t in range(NT):
                    ag = nc.vector.bn_aggr(mean_var[:, t, :], stats[:, t, :])
                ag.then_inc(mv_done, 1)

            def take_over(e):
                if not (isinstance(e, int) and e == 0):
                    dve.wait_ge(added, 16 * NT * e)
                dve.wait_ge(rows_in, 16 * NT * (e + 1))
                nc.vector.tensor_copy(index[:], index_next[:])
                nc.vector.tensor_copy(weight[:], rows[:, :, bass.ds(e + C, 1)].rearrange("p t o -> p (t o)"))\
                    .then_inc(expert_set, 1)

            def expert(e, last):
                n0 = FF_PROLOGUE_ITEMS + FF_ITEMS * e
                for f in range(FT):
                    item_w2(n0 + f, f + 1, e, f)
                take_over(e)
                if not last:
                    make_list(e + 1)
                for t in range(NT):
                    dve.wait_ge(o_full, NT * e + t + 1)
                    if t == 0:
                        dve.wait_ge(b2_in, 16 * e + 16)
                    nc.vector.tensor_tensor(o[:, t, :], o_ps[:, t % 2, 0:C], b2[:], ALU.add).then_inc(o_biased, 1)
                    dve.wait_ge(o_biased, NT * e + t + 1)
                    nc.vector.tensor_scalar(o[:, t, :], o[:, t, :], weight[:, t:t + 1], None, ALU.mult)\
                        .then_inc(o_done, 1)
                    if not last:
                        item_w1(n0 + FT + t, FT + t + 1, e + 1, t)
                        if t == 0:
                            norm_stats(e + 1)
                if not last:
                    for k in range(KT):
                        item_y(n0 + FT + NT + k, FT + NT + k + 1, e + 1, k)

            flat = lambda tile: tile[:].rearrange("p e t -> p (e t)")
            wide = lambda tile: tile[:].unsqueeze(2).broadcast_to([P, E, TILES])
            nc.vector.memset(low[:], 0.0)
            nc.vector.memset(high[:], 1.0)
            nc.vector.memset(mid[:], 0.5)
            nc.vector.memset(both[:], 1.0).then_inc(round_step, 1)
            with dve.Fori(0, ROUNDS) as r:
                dve.wait_ge(round_step, 4 * r + 1)
                nc.vector.tensor_tensor(chosen[:], s_all[:], wide(both), ALU.is_ge).then_inc(tested, 1)
                dve.wait_ge(counted, r + 1)
                nc.vector.tensor_reduce(count[:], count_ps[:, 0, :].rearrange("p (e t) -> p e t", e=E), AX.X, ALU.add)\
                    .then_inc(round_step, 1)
                dve.wait_ge(round_step, 4 * r + 2)
                nc.vector.scalar_tensor_tensor(out=low_try[:], in0=count[:], scalar=K - 0.5, in1=mid[:],
                                               op0=ALU.is_ge, op1=ALU.mult)
                nc.vector.scalar_tensor_tensor(out=high_try[:], in0=count[:], scalar=K - 0.5, in1=mid[:],
                                               op0=ALU.is_ge, op1=ALU.max).then_inc(round_step, 1)
                dve.wait_ge(round_step, 4 * r + 3)
                nc.vector.tensor_tensor(low[:], low[:], low_try[:], ALU.max)
                nc.vector.tensor_tensor(high[:], high[:], high_try[:], ALU.min).then_inc(round_step, 1)
                dve.wait_ge(round_step, 4 * r + 4)
                nc.vector.tensor_tensor(both[:], low[:], high[:], ALU.add).then_inc(round_step, 1)
                dve.wait_ge(round_step, 4 * r + 5)
                nc.vector.tensor_scalar(mid[:], both[:], 0.5, None, ALU.mult)
            nc.vector.tensor_tensor(thr[:], low[:], low[:], ALU.add).then_inc(route, 1)
            dve.wait_ge(route, 1)
            nc.vector.tensor_tensor(above[:], s_all[:], wide(thr), ALU.is_gt).then_inc(route, 1)
            nc.vector.tensor_tensor(tied[:], s_all[:], wide(thr), ALU.is_equal).then_inc(route, 1)
            dve.wait_ge(route_ps, 1)
            nc.vector.tensor_reduce(count[:], count_ps[:, 0, :].rearrange("p (e t) -> p e t", e=E), AX.X, ALU.add)\
                .then_inc(route, 1)
            dve.wait_ge(route, 4)
            nc.vector.tensor_scalar(room[:], count[:], -1.0, float(K), ALU.mult, ALU.add).then_inc(route, 1)
            nc.vector.memset(not_first[:], 1.0).then_inc(route, 1)
            dve.wait_ge(route, 6)
            nc.vector.memset(not_first[:, :, 0:1], 0.0).then_inc(route, 1)
            dve.wait_ge(route, 7)

            def ranks(step, n):
                dve.wait_ge(route_ps, n)
                nc.vector.tensor_tensor_scan(flat(scan), flat(not_first), count_ps[:, 1, :], 0.0, ALU.mult, ALU.add)\
                    .then_inc(route, 1)
                dve.wait_ge(route, step + 1)
                nc.vector.tensor_tensor(flat(tmp), flat(scan), count_ps[:, 1, :], ALU.subtract).then_inc(route, 1)
                dve.wait_ge(route, step + 2)
                nc.vector.tensor_tensor(flat(place), flat(tmp), count_ps[:, 0, :], ALU.add).then_inc(route, 1)
                dve.wait_ge(route, step + 3)

            ranks(7, 2)
            nc.vector.tensor_tensor(tmp[:], place[:], wide(room), ALU.is_le).then_inc(route, 1)
            dve.wait_ge(route, 11)
            nc.vector.tensor_tensor(tmp[:], tmp[:], tied[:], ALU.mult).then_inc(route, 1)
            dve.wait_ge(route, 12)
            nc.vector.tensor_tensor(chosen[:], tmp[:], above[:], ALU.add).then_inc(route, 1)
            ranks(CHOSEN_STEP, 3)
            nc.vector.tensor_tensor(tmp[:], place[:], chosen[:], ALU.mult).then_inc(route, 1)
            dve.wait_ge(route, 17)
            nc.vector.tensor_scalar(place[:], tmp[:], -1.0, None, ALU.add).then_inc(route, 1)
            dve.wait_ge(route, 18)
            dve.wait_ge(consts, 3)
            dve.wait_ge(item_full, 1)
            nc.vector.tensor_copy(b1T[:], transpose_ps[:, 0, 0:E * FT]).then_inc(item_free, 1)
            for t in range(NT):
                item_w1(1 + t, 1 + t, 0, t)
            make_list(0)
            norm_stats(0)
            dve.wait_ge(small_in, 48)
            for k in range(KT):
                item_y(1 + NT + k, 1 + NT + k, 0, k)
            expert(0, False)
            with dve.Fori(1, E - 1) as e:
                expert(e, False)
            expert(E - 1, True)

        @block.gpsimd
        def _(pool):
            idle = itertools.cycle(range(1, 17))

            def hold():
                c = next(idle)
                nc.gpsimd.tensor_tensor(pool_idle[:, c:c + 1], pool_idle[:, 0:1], pool_idle[:, 0:1], ALU.add)

            def gather(e):
                pool.wait_ge(list_full, 2 * e + 2)
                if not (isinstance(e, int) and e == 0):
                    pool.wait_ge(expert_set, e)
                hold()
                for t in range(NT):
                    pool.indirect_dma_start(
                        out=rows[:, t, :], out_offset=None, in_=z_flat,
                        in_offset=bass.IndirectOffsetOnAxis(ap=index_next[:, t:t + 1].bitcast(U32), axis=0))\
                        .then_inc(rows_in, 16)

            def normalize(e):
                pool.wait_ge(mv_done, e + 1)
                hold()
                nc.gpsimd.tensor_scalar(rstd[:], mean_var[:, :, 1], EPS, None, ALU.add).then_inc(rstd_step, 1)
                pool.wait_ge(rstd_step, 2 * e + 1)
                nc.gpsimd.tensor_tensor(rstd[:], rstd[:], minus_half[:], ALU.pow).then_inc(rstd_step, 1)
                pool.wait_ge(rstd_step, 2 * e + 2)
                hold()
                for t in range(NT):
                    nz = nc.gpsimd.tensor_scalar(y[:, t, :], rows[:, t, 0:C], mean_var[:, t, 0:1], rstd[:, t:t + 1],
                                                 ALU.subtract, ALU.mult)
                nz.then_inc(y_done, 1)

            def scatter(e):
                for t in range(NT):
                    pool.wait_ge(o_done, NT * e + t + 1)
                    hold()
                    pool.indirect_dma_start(
                        out=out_flat, out_offset=bass.IndirectOffsetOnAxis(ap=index[:, t:t + 1].bitcast(U32), axis=0),
                        in_=o[:, t, :], in_offset=None, compute_op=ALU.add).then_inc(added, 16)

            nc.gpsimd.memset(ident[:], 0.0)
            nc.gpsimd.memset(ones[:], 1.0)
            nc.gpsimd.memset(upto[:], 1.0)
            nc.gpsimd.memset(minus_half[:], -0.5)
            nc.gpsimd.memset(pool_idle[:], 0.0).then_inc(pool_set, 1)
            pool.wait_ge(pool_set, 1)
            nc.gpsimd.affine_select(out=ident[:], in_=ident[:], compare_op=ALU.not_equal, fill=1.0, base=0,
                                    pattern=[[-1, P]], channel_multiplier=1).then_inc(consts, 1)
            nc.gpsimd.affine_select(out=upto[:], in_=upto[:], compare_op=ALU.is_ge, fill=0.0, base=0,
                                    pattern=[[1, P]], channel_multiplier=-1).then_inc(consts, 1)
            nc.gpsimd.iota(iota[:], pattern=[[1, P]], base=0, channel_multiplier=0, allow_small_or_imprecise_dtypes=True)
            nc.gpsimd.iota(token[:, 0, :], pattern=[[1, TILES]], base=0, channel_multiplier=0,
                           allow_small_or_imprecise_dtypes=True)
            nc.gpsimd.iota(token[:, 1, :], pattern=[[0, TILES]], base=0, channel_multiplier=1,
                           allow_small_or_imprecise_dtypes=True).then_inc(consts, 1)
            gather(0)
            normalize(0)
            with pool.Fori(0, E - 1) as e:
                gather(e + 1)
                normalize(e + 1)
                scatter(e)
            scatter(E - 1)
            pool.wait_ge(added, 16 * NT * E)


CHOSEN_STEP = 13
LIST_STEPS = 2 * 4 + 1


def kernel(**inputs):
    import numpy as np
    import concourse.bacc as bacc
    from concourse.bass_utils import run_bass_kernel_spmd

    nc = bacc.Bacc("TRN2", target_bir_lowering=False, num_devices=1)
    arrays, ins, w = {}, {}, {}
    for name in inputs:
        a = np.ascontiguousarray(inputs[name])
        arrays[f"in_{name}"] = a
        ins[name] = nc.dram_tensor(f"in_{name}", a.shape, mybir.dt.from_np(a.dtype), kind="ExternalInput").ap()
        if name.startswith("L0_"):
            w[name.split("_", 2)[2]] = ins[name]
    shape = inputs["x"].shape
    out = nc.dram_tensor("out", shape, F32, kind="ExternalOutput").ap()
    program(nc, ins["x"], ins["ctx_512"], w, out)
    r = run_bass_kernel_spmd(nc, [arrays], core_ids=[0])
    return r.results[0]["out"]


def program(nc, x, ctx_in, w, out, z_rows=None):
    B, T, C = x.shape
    E = w["gate_w"].shape[0]
    if z_rows is None:
        z_rows = nc.dram_tensor("z_rows", (B, T, C + E), F32).ap()
    parts_dram = nc.dram_tensor("parts_dram", (2, 3, P, Q_COLS + K_COLS), BF16).ap()
    shift_dram = nc.dram_tensor("shift_dram", (2, SHIFT_ROWS, UH * Q_COLS), BF16).ap()
    with nc.sbuf_tensor("s_all", [P, E, B * T // P], F32) as s_all:
        attention(nc, x, ctx_in, w, z_rows, out, parts_dram, shift_dram, s_all)
        feed_forward(nc, w, z_rows, out, s_all)
```

```python
import itertools
from contextlib import ExitStack

import concourse.bass as bass
from concourse import mybir

F32 = mybir.dt.float32
BF16 = mybir.dt.bfloat16
I32 = mybir.dt.int32
U32 = mybir.dt.uint32
ALU = mybir.AluOpType
ACT = mybir.ActivationFunctionType
AX = mybir.AxisListType

P = 128
H, D = 16, 16
UH = 4
UNITS = H // UH
HALF_H = P // D
Q_PART = (0, 0, 1, 0, 2, 1)
K_PART = (0, 1, 0, 2, 0, 1)
ROWS = len(Q_PART) * D
SHIFT_ROWS = 2
KROWS = ROWS + SHIFT_ROWS
SCALE = float(D) ** -0.5
EPS = 1e-5
NEG = -1e30
TWO_ONES = 1.0 + 0x3f80 * 2.0 ** -23
CROSS_IT = 8
ITS = 12
A_PER_IT = 4
N_A = ITS * A_PER_IT
N_EXP = 2 * ITS


def pieces(first, last):
    at = {}
    for g in range(UNITS):
        if not (last and g == 3):
            at[g, 0] = "shift"
        if not (first and g == 0):
            at[g, 2] = "out_self"
        at[g, 10] = "out_cross"
    if not first:
        at.update({(0, 1): "v", (0, 3): "vc0", (0, 4): "vc1", (0, 6): "yT0", (0, 7): "yT1",
                   (1, 8): "proj0", (1, 9): "proj1", (2, 6): "zT0", (2, 7): "zT1", (2, 9): "gate"})
    if not last:
        at.update({(0, 8): "y0T0", (0, 9): "y0T1", (0, 5): "ctxT0", (0, 11): "ctxT1",
                   (1, 1): "q", (1, 3): "qc", (1, 4): "k", (1, 5): "kc0", (1, 6): "kc1",
                   (2, 3): "v", (2, 4): "vc0", (2, 5): "vc1",
                   (2, 11): "q", (3, 1): "qc", (3, 3): "k", (3, 4): "kc0", (3, 5): "kc1"})
    return dict(sorted(at.items()))


HALF_PIECES = ("q", "qc", "k", "kc0", "kc1")
V_PIECES = ("v", "vc0", "vc1")
PROLOGUE = (("ctxT0", 0), ("ctxT1", 0), ("y0T0", 0), ("y0T1", 0), *((n, 0) for n in HALF_PIECES),
            *((n, 0) for n in V_PIECES), ("gateT", 0),
            *((n, 1) for n in V_PIECES), *((n, 1) for n in HALF_PIECES))
ALONE = PROLOGUE.index(("qc", 1))
UNWEIGHTED = 4
PIECE_EVERY = 5
READ_LATER = 2
BANKS = 4


def piece_beside(a):
    n = ALONE + a // PIECE_EVERY
    return n if a >= 0 and a % PIECE_EVERY == 0 and n < len(PROLOGUE) else None


EPILOGUE = ("out_self", "yT0", "yT1", "proj0", "proj1", "zT0", "zT1", "gate")
COL = {"q": (0, 512), "qc": (512, 1024), "k": (1024, 1536), "kc0": (1536, 2048), "kc1": (2048, 2560)}
BIAS = {"q": 0, "qc": 1, "k": 2, "kc0": 3, "kc1": 3}
Q_COLS, K_COLS = 1024, 1536


def half_of(name, g):
    if name in V_PIECES:
        return 1 if g == 0 else 0
    return 0 if g == 1 else 1


def piece_number(b, first, last, g, i):
    order = list(pieces(first, last))
    n = len(PROLOGUE) + 1 + order.index((g, i))
    if not first:
        n = n + len(pieces(True, False)) + (b - 1) * len(pieces(False, False))
    return n


class Unit:

    def __init__(self, b, g):
        self.b, self.g = b, g

    def __radd__(self, n):
        return n + UNITS * self.b + self.g

    __add__ = __radd__

    def __rmul__(self, n):
        return n * UNITS * self.b + n * self.g


def unit_parity(unit):
    return unit.g % 2


def unit_group(unit):
    return unit.g


def piece_args(name, b, g):
    if name == "shift":
        unit = Unit(b, g + 1) if g < UNITS - 1 else Unit(b + 1, 0)
    elif name == "out_self":
        unit = Unit(b, g - 1) if g else Unit(b - 1, UNITS - 1)
    else:
        unit = Unit(b, g)
    if name in ("yT0", "yT1", "proj0", "proj1", "zT0", "zT1", "gate"):
        return b - 1, 0, unit
    return b + 1, half_of(name, g), unit


def projection(name, b, g):
    if name not in COL:
        return None
    halves = 2 * b + 2 + half_of(name, g)
    return 10 * b + 10 + 5 * half_of(name, g) + HALF_PIECES.index(name), halves


def rest_place(name, hf):
    return (5 * hf + HALF_PIECES.index(name)) % 2


_CROSS = [("cross", h, t, c) for h in range(UH) for t in range(4) for c in range(2)]
_SELF = [("self", h, t, 0) for h in range(UH) for t in range(4)]
MAX_ORDER = [m for n in range(16) for m in (_CROSS[2 * n], _CROSS[2 * n + 1], _SELF[n])]


def attention(nc, x, ctx_in, w, z_rows, out, parts_dram, shift_dram, s_all):
    B, T, C = x.shape
    TC, CC = ctx_in.shape[1:]
    KT = C // P
    NT = T // P
    NC_T = TC // P
    E = w["gate_w"].shape[0]
    assert T == 512 and C == 2 * P and CC == P and NC_T == CROSS_IT and NT + CROSS_IT == ITS

    with ExitStack() as stack:
        def sb(name, shape, dt=F32):
            return stack.enter_context(nc.sbuf_tensor(name, shape, dt))

        def ps(name, shape):
            return stack.enter_context(nc.psum_tensor(name, shape, F32))

        def sem(name):
            return stack.enter_context(nc.semaphore(name))

        q_stack = sb("q_stack", [P, UNITS, UH, Q_COLS], BF16)
        k_stack = sb("k_stack", [P, UNITS, UH, K_COLS], BF16)
        probs = sb("probs", [P, 4, 2, T])
        parts = sb("parts", [P, 3, Q_COLS + K_COLS], BF16)
        rest = sb("rest", [P, 2, T])
        x_sb = sb("x_sb", [P, NT, C])
        c_sb = sb("c_sb", [P, NC_T, CC])
        y0T = sb("y0T", [P, KT, T])
        ctxT = sb("ctxT", [P, TC])
        v_self = sb("v_self", [P, 2, NT, HALF_H, 32])
        v_cross = sb("v_cross", [P, 2, NC_T, HALF_H, 32])
        w_q = sb("w_q", [P, KT, C]); w_k = sb("w_k", [P, KT, C]); w_v = sb("w_v", [P, KT, C])
        w_cq = sb("w_cq", [P, KT, C]); w_p = sb("w_p", [P, KT, C])
        w_ck = sb("w_ck", [P, C]); w_cv = sb("w_cv", [P, C])
        bias = sb("bias", [P, 4, 2])
        bias_v = sb("bias_v", [P, 3, KT])
        bias_p = sb("bias_p", [P, C])
        gate_n = sb("gate_n", [E, C])
        gateT = sb("gateT", [P, KT, E])
        u_sb = sb("u_sb", [P, 2, T])
        y_sb = sb("y_sb", [P, NT, C])
        y_add = sb("y_add", [P, NT, UH, D])
        rden = sb("rden", [P, 2, NT, UH])
        yT = sb("yT", [P, KT, T])
        x1 = sb("x1", [P, NT, C])
        z_sb = sb("z_sb", [P, NT, C + E])
        zT = sb("zT", [P, KT, T])
        th = sb("th", [P, NT, E])
        stats = sb("stats", [P, 2, NT, 6])
        mean_var = sb("mean_var", [P, 2, NT, 2])
        rstd = sb("rstd", [P, 2, NT])
        minus_half = sb("minus_half", [P, NT])
        ident = sb("ident", [P, P])
        ident_16 = sb("ident_16", [P, P], BF16)
        causal = sb("causal", [P, P], BF16)
        chunk_max = sb("chunk_max", [P, UH * NT, 2])
        row_max = sb("row_max", [P, 2, UH, 2, NT])
        pool_idle = sb("pool_idle", [P, 17])
        dve_idle = sb("dve_idle", [P, 1])
        shift = sb("shift", [2 * UH * NT, 2, P], BF16)

        score_ps = ps("score_ps", [P, 4, T])
        max_ps = ps("max_ps", [P, 2, T])
        out_ps = ps("out_ps", [P, T])
        piece_ps = ps("piece_ps", [P, T])

        weights_in = sem("weights_in")
        consts = sem("consts")
        x_in = sem("x_in"); c_in = sem("c_in"); xr_in = sem("xr_in")
        stats_done = [sem("stats0_done"), sem("stats1_done")]
        mv_done = [sem("mv0_done"), sem("mv1_done")]
        rstd_step = [sem("rstd0_step"), sem("rstd1_step")]
        ln_done = [sem("ln0_done"), sem("ln1_done")]
        piece_full = sem("piece_full")
        piece_free = sem("piece_free")
        read_by_act = sem("read_by_act"); read_by_dve = sem("read_by_dve")
        high_done = sem("high_done")
        mid_done = sem("mid_done")
        low_done = sem("low_done")
        parts_out = sem("parts_out")
        slot_in = [sem(f"slot_in{s}") for s in range(UNITS)]
        shift_high = sem("shift_high")
        maxin_ready = sem("maxin_ready")
        max_done = sem("max_done")
        rowmax_done = sem("rowmax_done")
        shift_out = sem("shift_out")
        shift_in = [sem(f"shift_in{s}") for s in range(UNITS)]
        scores_ready = sem("scores_ready")
        exp_done = sem("exp_done")
        mask_done = sem("mask_done")
        pv_done = sem("pv_done")
        u_ready = sem("u_ready")
        rden_done = sem("rden_done")
        y_part = sem("y_part"); y_done = sem("y_done")
        pool_set = sem("pool_set"); ones_set = sem("ones_set")
        xb_done = sem("xb_done")
        v_bias_done = sem("v_bias_done")
        expert_scores = sem("expert_scores")
        base_done = sem("base_done")
        z_out = sem("z_out"); base_out = sem("base_out")

        N_LOADS = 15

        END = piece_number(B - 1, False, True, 0, 0) + len(pieces(False, True))

        block = stack.enter_context(nc.Block())

        def freed(n):
            if not (isinstance(n, int) and n < len(PROLOGUE)):
                return piece_free, n + 1 - len(PROLOGUE)
            split = PROLOGUE[n][0] in COL
            return (read_by_dve if split else read_by_act), sum((m in COL) == split for m, _ in PROLOGUE[:n + 1])

        def piece_bank(n):
            return score_ps[:, n % BANKS] if isinstance(n, int) and n < len(PROLOGUE) else piece_ps

        FILL = 16 * 2 * len(Q_PART)
        PARTS = 16 * len(HALF_PIECES)
        LOADS = 16 * N_LOADS

        def tokens(dram, n):
            return dram[n].rearrange("(t p) c -> p t c", p=P)

        @block.sync
        def _(sp):
            def load_inputs(n):
                sp.dma_start(x_sb[:], tokens(x, n)).then_inc(x_in, 16)
                sp.dma_start(c_sb[:], tokens(ctx_in, n)).then_inc(c_in, 16)

            def load_weights():
                for name, tile in (("Wq", w_q), ("Wcq", w_cq), ("Wk", w_k), ("Wv", w_v), ("Wp", w_p)):
                    sp.dma_start(tile[:], w[name].rearrange("(t p) c -> p t c", p=P)).then_inc(weights_in, 16)
                for name, tile in (("Wck", w_ck), ("Wcv", w_cv)):
                    sp.dma_start(tile[:], w[name]).then_inc(weights_in, 16)
                for n, name in enumerate(("bq", "bcq", "bk", "bck")):
                    sp.dma_start(bias[:, n, :], w[name].rearrange("(t p) -> p t", p=P),
                                 allow_slow_non_contiguous=True).then_inc(weights_in, 16)
                for n, name in enumerate(("bv", "bcv")):
                    sp.dma_start(bias_v[:, n, :], w[name].rearrange("(t p) -> p t", p=P),
                                 allow_slow_non_contiguous=True).then_inc(weights_in, 16)
                sp.dma_start(bias_p[:], w["bp"].rearrange("(o c) -> o c", o=1).broadcast_to([P, C]))\
                    .then_inc(weights_in, 16)
                sp.dma_start(gate_n[:], w["gate_w"]).then_inc(weights_in, 16)

            def store_parts(hf, name, number, stacked=None):
                a, e = COL[name]
                sp.wait_ge(low_done, number)
                if stacked is not None and name == HALF_PIECES[0]:
                    for slot in (2 * hf, 2 * hf + 1):
                        sp.wait_ge(slot_in[slot], stacked)
                sp.dma_start(parts_dram[hf, :, :, a:e].rearrange("t c n -> c t n"), parts[:, :, a:e])\
                    .then_inc(parts_out, 16)

            def fill(slot, halves):
                hf, at = slot // 2, slot % 2 * UH * D
                sp.wait_ge(parts_out, PARTS * halves)
                for r in range(len(Q_PART)):
                    rows = slice(D * r, D * r + D)
                    sp.dma_start(q_stack[rows, slot], parts_dram[hf, Q_PART[r], at:at + UH * D, 0:Q_COLS]
                                 .rearrange("(h d) n -> d h n", d=D)).then_inc(slot_in[slot], 16)
                    sp.dma_start(k_stack[rows, slot], parts_dram[hf, K_PART[r], at:at + UH * D, Q_COLS:]
                                 .rearrange("(h d) n -> d h n", d=D)).then_inc(slot_in[slot], 16)

            def put_shift(slot, number, piece):
                sp.wait_ge(*freed(piece))
                sp.dma_start(shift_dram[slot % 2].rearrange("t (r q) -> r t q", q=P), shift[:])\
                    .then_inc(shift_out, 16)
                sp.wait_ge(shift_out, 16 * number + 16)
                sp.dma_start(q_stack[ROWS:KROWS, slot].rearrange("p h n -> p (h n)"), shift_dram[slot % 2])\
                    .then_inc(shift_in[slot], 16)

            def store_results(n, done):
                sp.wait_ge(expert_scores, done)
                sp.dma_start(tokens(z_rows, n), z_sb[:]).then_inc(z_out, 16)
                sp.wait_ge(base_done, done)
                sp.dma_start(tokens(out, n), x1[:]).then_inc(base_out, 16)

            def stored(batches):
                sp.wait_ge(z_out, 16 * batches)
                sp.wait_ge(base_out, 16 * batches)

            def load_residual(n):
                sp.dma_start(x1[:], tokens(x, n)).then_inc(xr_in, 16)

            def batch(b, first, last):
                before, after = (b - 1, b + 1) if isinstance(b, int) else (sp.snap(b - 1), sp.snap(b + 1))
                for g in range(UNITS):
                    if g == 0 and not last:
                        sp.wait_ge(*freed(piece_number(b, first, last, 0, 0) - 1))
                        load_inputs(after)
                    if g == 0 and first:
                        load_residual(b)
                    if not (last and g == 3):
                        put_shift((g + 1) % UNITS, 4 * b + g + 1, piece_number(b, first, last, g, 0))
                    if not last and g in (1, 3):
                        hf = g // 2
                        for n, name in enumerate(HALF_PIECES):
                            store_parts(hf, name, 10 * b + 10 + 5 * hf + n + 1, FILL * b + FILL)
                        sp.wait_ge(scores_ready, N_EXP * (4 * b + 2 * hf + 1))
                        fill(2 * hf, 2 * b + 3 + hf)
                    if not last and g in (2,):
                        sp.wait_ge(scores_ready, N_EXP * (4 * b + 2))
                        fill(1, 2 * b + 3)
                    if not first and g == 0:
                        sp.wait_ge(scores_ready, N_EXP * (4 * b))
                        fill(3, 2 * b + 2)
                    if not first and g == 2:
                        store_results(before, b)
                        stored(b)
                        load_residual(b)

            load_inputs(0)
            load_weights()
            for hf in range(2):
                for n, name in enumerate(HALF_PIECES):
                    store_parts(hf, name, 5 * hf + n + 1)
                fill(2 * hf, hf + 1)
                fill(2 * hf + 1, hf + 1)
            put_shift(0, 0, len(PROLOGUE))
            batch(0, True, False)
            with sp.Fori(1, B - 1) as b:
                batch(b, False, False)
            batch(B - 1, False, True)
            store_results(B - 1, B)
            stored(B)

        def score_span(i):
            if i < CROSS_IT:
                return 0, T, T + i * P
            return (i - CROSS_IT) * P, 0, (i - CROSS_IT) * P

        @block.tensor
        def _(pe):
            def score_pair(b, g, i, p):
                u = UNITS * b + g
                if not (isinstance(b, int) and u == 0 and i == 0):
                    pe.wait_ge(exp_done, N_EXP * u + 2 * i + p - 1)
                if i == 0 and p == 0:
                    pe.wait_ge(shift_in[g], 16 * b + 16)
                q0, qc, kc = score_span(i)
                for h in (2 * p, 2 * p + 1):
                    mm = pe.matmul(score_ps[:, h, q0:T], k_stack[0:KROWS, g, h, kc:kc + P],
                                   q_stack[0:KROWS, g, h, qc + q0:qc + T], start=True, stop=True)
                mm.then_inc(scores_ready, 1)

            def values(b, g, i, part):
                u = UNITS * b + g
                if part == 0 and i < CROSS_IT:
                    pe.wait_ge(exp_done, N_EXP * u + 2 * i + 2)
                elif part == 0:
                    pe.wait_ge(mask_done, 2 * NT * u + 2 * (i - CROSS_IT) + 2)
                if part == 0 and i in (0, CROSS_IT) and not (isinstance(b, int) and u == 0 and i == 0):
                    pe.wait_ge(u_ready, 2 * u + (i > 0))
                q0 = score_span(i)[0]
                v, kt = (v_cross, i) if i < CROSS_IT else (v_self, i - CROSS_IT)
                middle = T if kt == 0 else (q0 + T) // 2
                if part == 1 and kt == 0:
                    return
                cols = slice(middle, T) if part else slice(q0, middle)
                for h in range(UH):
                    mm = pe.matmul(out_ps[32 * h:32 * h + 32, cols], v[:, g // 2, kt, g % 2 * UH + h, :],
                                   probs[:, i % 2 * 2 + h // 2, h % 2, cols],
                                   start=kt == 0, stop=part == 1 and i in (CROSS_IT - 1, ITS - 1))
                if part == 1 or kt == 0:
                    mm.then_inc(pv_done, 1)

            def max_input(b, g, a):
                u = UNITS * b + g
                kind, h, qt, chunk = MAX_ORDER[a]
                if a == 0:
                    pe.wait_ge(slot_in[g], FILL * b + FILL)
                if not (isinstance(b, int) and u == 0 and a < 2):
                    pe.wait_ge(max_done, N_A * u + a - 1)
                if kind == "cross":
                    qc, k0, n = T + qt * P, T + chunk * T, T
                else:
                    qc, k0, n = qt * P, 0, (qt + 1) * P
                mm = pe.matmul(max_ps[:, a % 2, 0:n], q_stack[0:ROWS, g, h, qc:qc + P],
                               k_stack[0:ROWS, g, h, k0:k0 + n], start=True, stop=kind == "cross")
                if kind == "self":
                    mm = pe.matmul(max_ps[:, a % 2, n - P:n], ident_16[:], causal[:], start=False, stop=True)
                mm.then_inc(maxin_ready, 1)

            def transpose4(bank, sources):
                for n, src in enumerate(sources):
                    mm = pe.transpose(bank[:, n * P:(n + 1) * P], src, ident[:])
                return mm

            def product(dst, pairs):
                for n, (lhs, rhs) in enumerate(pairs):
                    mm = pe.matmul(dst, lhs, rhs, start=n == 0, stop=n == len(pairs) - 1)
                return mm

            def piece(name, n, b, hf, unit):
                bank = piece_bank(n)
                if bank is not piece_ps:
                    if n >= BANKS:
                        pe.wait_ge(*freed(n - BANKS))
                elif not (isinstance(n, int) and n == len(PROLOGUE)):
                    pe.wait_ge(*freed(n - 1))
                c = int(name[-1]) if name[-1].isdigit() else 0
                cols = slice(hf * P, hf * P + P)
                if name == "gateT":
                    for t in range(KT):
                        mm = pe.transpose(bank[:, t * E:(t + 1) * E], gate_n[:, t * P:(t + 1) * P], ident[0:E, 0:E])
                elif name == "shift":
                    pe.wait_ge(rowmax_done, unit + 1)
                    mm = pe.transpose(bank[0:2 * UH * NT, 0:P],
                                      row_max[:, unit_parity(unit)].rearrange("p h s t -> p (h s t)"), ident[:])
                elif name in ("out_cross", "out_self"):
                    s = int(name == "out_self")
                    pe.wait_ge(u_ready, 2 * unit + s + 1)
                    mm = transpose4(bank, [u_sb[:, s, t * P:(t + 1) * P] for t in range(NT)])
                elif name in ("yT0", "yT1"):
                    pe.wait_ge(y_done, UNITS * b + UNITS)
                    mm = transpose4(bank, [y_sb[:, t, c * P:(c + 1) * P] for t in range(NT)])
                elif name in ("proj0", "proj1"):
                    for t in (0, 1):
                        tok = slice((2 * c + t) * P, (2 * c + t + 1) * P)
                        mm = product(bank[:, t * C:(t + 1) * C], [(yT[:, k, tok], w_p[:, k, :]) for k in range(KT)])
                elif name in ("zT0", "zT1"):
                    pe.wait_ge(ln_done[1], b + 1)
                    mm = transpose4(bank, [z_sb[:, t, c * P:(c + 1) * P] for t in range(NT)])
                elif name == "gate":
                    for t in range(NT):
                        mm = product(bank[:, t * E:(t + 1) * E],
                                     [(zT[:, k, t * P:(t + 1) * P], gateT[:, k, :]) for k in range(KT)])
                elif name in ("y0T0", "y0T1"):
                    pe.wait_ge(ln_done[0], b + 1)
                    mm = transpose4(bank, [x_sb[:, t, c * P:(c + 1) * P] for t in range(NT)])
                elif name in ("ctxT0", "ctxT1"):
                    pe.wait_ge(c_in, 16 * b + 16)
                    mm = transpose4(bank, [c_sb[:, NT * c + t, :] for t in range(NT)])
                elif name in ("q", "qc", "k"):
                    wt = {"q": w_q, "qc": w_cq, "k": w_k}[name]
                    mm = product(bank[:], [(wt[:, k, cols], y0T[:, k, :]) for k in range(KT)])
                elif name in ("kc0", "kc1"):
                    mm = product(bank[:], [(w_ck[:, cols], ctxT[:, c * T:(c + 1) * T])])
                elif name == "v":
                    for t in range(NT):
                        mm = product(bank[:, t * P:(t + 1) * P],
                                     [(y0T[:, k, t * P:(t + 1) * P], w_v[:, k, cols]) for k in range(KT)])
                elif name in ("vc0", "vc1"):
                    for t in range(NT):
                        tok = slice((NT * c + t) * P, (NT * c + t + 1) * P)
                        mm = product(bank[:, t * P:(t + 1) * P], [(ctxT[:, tok], w_cv[:, cols])])
                mm.then_inc(piece_full, 1)

            def batch(b, first, last):
                at = pieces(first, last)
                for g in range(UNITS):
                    for i in range(ITS):
                        ahead = not (last and g >= 2)
                        to = (b, g + 2) if g < 2 else (b + 1, g - 2)
                        before = (b, g, i - 1) if i else (b, g - 1, ITS - 1) if g else (b - 1, UNITS - 1, ITS - 1)
                        for n in range(A_PER_IT):
                            if ahead:
                                max_input(*to, A_PER_IT * i + n)
                            if n < 2:
                                score_pair(b, g, i, n)
                            elif not (first and g == 0 and i == 0):
                                values(*before, n - 2)
                            if n == A_PER_IT - 1 and (g, i) in at:
                                piece(at[g, i], piece_number(b, first, last, g, i), *piece_args(at[g, i], b, g))

            pe.wait_ge(consts, 3)
            for n, (name, hf) in enumerate(PROLOGUE[:ALONE]):
                if n == UNWEIGHTED:
                    pe.wait_ge(weights_in, LOADS)
                    pe.wait_ge(*freed(n - 1))
                piece(name, n, 0, hf, 0)
            for a in range(N_A):
                max_input(0, 0, a)
                n = piece_beside(a)
                if n is not None:
                    piece(PROLOGUE[n][0], n, 0, PROLOGUE[n][1], 0)
            for name in ("kc1", "vc1"):
                pe.wait_ge(*freed(PROLOGUE.index((name, 1))))
            piece("shift", len(PROLOGUE), 0, 0, Unit(0, 0))
            for a in range(N_A):
                max_input(0, 1, a)
            pe.wait_ge(ones_set, 1)
            batch(0, True, False)
            with pe.Fori(1, B - 1) as b:
                batch(b, False, False)
            batch(B - 1, False, True)
            for part in range(2):
                values(B - 1, UNITS - 1, ITS - 1, part)
            for n, name in enumerate(EPILOGUE):
                piece(name, END + n, B - 1, 0, Unit(B - 1, UNITS - 1))

        @block.scalar
        def _(act):
            def exp_pair(b, g, i, p):
                u = UNITS * b + g
                q0 = score_span(i)[0]
                act.wait_ge(scores_ready, N_EXP * u + 2 * i + p + 1)
                if not (isinstance(b, int) and u == 0 and i < 2):
                    act.wait_ge(pv_done, ITS * u + i - 1)
                nc.scalar.activation(probs[:, i % 2 * 2 + p, :, q0:T], score_ps[:, 2 * p:2 * p + 2, q0:T],
                                     ACT.Exp, scale=SCALE).then_inc(exp_done, 1)

            def copy_out(b, g, s):
                u = UNITS * b + g
                act.wait_ge(pv_done, ITS * u + (ITS if s else CROSS_IT))
                if s == 0 and not (isinstance(b, int) and u == 0):
                    act.wait_ge(y_part, 2 * u - 1)
                elif s == 1:
                    act.wait_ge(y_part, 2 * u)
                nc.scalar.copy(u_sb[:, s, :], out_ps[:]).then_inc(u_ready, 1)

            def piece(name, n, b, hf, unit, k):
                c = int(name[-1]) if name[-1].isdigit() else 0
                if name in ("out_cross", "out_self", "proj0", "proj1"):
                    return
                bank = piece_bank(n)
                act.wait_ge(piece_full, n + 1)
                if name == "gateT":
                    nc.scalar.copy(gateT[:].rearrange("p t e -> p (t e)"), bank[:, 0:KT * E]).then_inc(freed(n)[0], 1)
                elif name == "shift":
                    act.wait_ge(shift_out, 16 * unit)
                    nc.scalar.mul(shift[:, 0, :], bank[0:2 * UH * NT, 0:P], -1.0).then_inc(shift_high, 1)
                elif name in ("yT0", "yT1"):
                    nc.scalar.activation(yT[:, c, :], bank[:], ACT.Identity, bias=bias_v[:, 2, c:c + 1])\
                        .then_inc(freed(n)[0], 1)
                elif name in ("zT0", "zT1", "y0T0", "y0T1"):
                    dst = (y0T if name[0] == "y" else zT)[:, c, :]
                    nc.scalar.copy(dst, bank[:]).then_inc(freed(n)[0], 1)
                elif name in ("ctxT0", "ctxT1"):
                    nc.scalar.copy(ctxT[:, c * T:(c + 1) * T], bank[:]).then_inc(freed(n)[0], 1)
                elif name == "gate":
                    nc.scalar.activation(th[:].rearrange("p t e -> p (t e)"), bank[:, 0:NT * E], ACT.Tanh)\
                        .then_inc(freed(n)[0], 1)
                elif name in COL:
                    a, e = COL[name]
                    halves = k[1]
                    if not (isinstance(halves, int) and halves == 0):
                        act.wait_ge(parts_out, PARTS * halves)
                    nc.scalar.activation(parts[:, 0, a:e], bank[:], ACT.Identity,
                                         bias=bias[:, BIAS[name], hf:hf + 1]).then_inc(high_done, 1)
                else:
                    v = (v_self if name == "v" else v_cross)[:, hf, NT * c:NT * c + NT, :, 0:D]
                    nc.scalar.copy(v, bank[:].rearrange("p (t h d) -> p t h d", t=NT, d=D)).then_inc(freed(n)[0], 1)

            def batch(b, first, last):
                at = pieces(first, last)
                for g in range(UNITS):
                    for i in range(ITS):
                        gi = (g, i - 1) if i else (g - 1, ITS - 1)
                        if gi in at:
                            piece(at[gi], piece_number(b, first, last, *gi),
                                  *piece_args(at[gi], b, gi[0]), projection(at[gi], b, gi[0]))
                        for p in range(2):
                            exp_pair(b, g, i, p)
                        if i == 0 and g > 0:
                            copy_out(b, g - 1, 1)
                        elif i == 0 and not first:
                            copy_out(b - 1, UNITS - 1, 1)
                        elif i == CROSS_IT:
                            copy_out(b, g, 0)

            for n, (name, hf) in enumerate(PROLOGUE):
                if n == UNWEIGHTED:
                    act.wait_ge(v_bias_done, 1)
                    act.wait_ge(consts, 3 + 1)
                piece(name, n, 0, hf, 0, (0, hf))
            piece("shift", len(PROLOGUE), 0, 0, Unit(0, 0), None)
            batch(0, True, False)
            with act.Fori(1, B - 1) as b:
                batch(b, False, False)
            batch(B - 1, False, True)
            copy_out(B - 1, UNITS - 1, 1)
            for n, name in enumerate(EPILOGUE):
                piece(name, END + n, B - 1, 0, Unit(B - 1, UNITS - 1), None)

        @block.vector
        def _(dve):
            def maximum(b, g, a):
                u = UNITS * b + g
                kind, h, qt, chunk = MAX_ORDER[a]
                bank = max_ps[:, a % 2]
                if a == 0 and not (isinstance(u, int) and u == 0):
                    dve.wait_ge(rowmax_done, u)
                n = T if kind == "cross" else (qt + 1) * P
                dst = (chunk_max[:, h * NT + qt, chunk:chunk + 1] if kind == "cross"
                       else row_max[:, g % 2, h, 0, qt:qt + 1])
                dve.wait_ge(maxin_ready, N_A * u + a + 1)
                nc.vector.tensor_reduce(dst, bank[:, 0:n], AX.X, ALU.max).then_inc(max_done, 1)

            def finish_maxima(b, g):
                u = UNITS * b + g
                dve.wait_ge(max_done, N_A * u + N_A)
                nc.vector.tensor_reduce(row_max[:, g % 2, :, 1, :], chunk_max[:].rearrange("p (h t) c -> p h t c", h=UH),
                                        AX.X, ALU.max).then_inc(rowmax_done, 1)

            def norm_stats(which, rows, count):
                for t in range(NT):
                    st = nc.vector.bn_stats(stats[:, which, t, :], rows(t))
                st.then_inc(stats_done[which], 1)
                dve.wait_ge(stats_done[which], count)
                nc.vector.memset(dve_idle[:], 0.0)
                for t in range(NT):
                    ag = nc.vector.bn_aggr(mean_var[:, which, t, :], stats[:, which, t, :])
                ag.then_inc(mv_done[which], 1)

            def piece(name, n, b, hf, unit, k):
                bank = piece_bank(n)
                if name == "shift":
                    dve.wait_ge(shift_high, unit + 1)
                    nc.vector.scalar_tensor_tensor(
                        out=shift[:, 1, :], in0=bank[0:2 * UH * NT, 0:P], scalar=-1.0, in1=shift[:, 0, :],
                        op0=ALU.mult, op1=ALU.subtract).then_inc(freed(n)[0], 1)
                elif name in ("out_cross", "out_self"):
                    s = int(name == "out_self")
                    g = unit_group(unit)
                    sums = bank[:].rearrange("p (t h d) -> p t h d", t=NT, h=UH)
                    dve.wait_ge(piece_full, n + 1)
                    nc.vector.reciprocal(rden[:, s], sums[:, :, :, D]).then_inc(rden_done, 1)
                    if s:
                        dve.wait_ge(y_done, unit + 0)
                        y = y_add[:]
                    else:
                        y = y_sb[:, :, g * UH * D:(g + 1) * UH * D].rearrange("p t (h d) -> p t h d", h=UH)
                    dve.wait_ge(rden_done, 2 * unit + s + 1)
                    nc.vector.tensor_tensor(y, sums[:, :, :, 0:D], rden[:, s].unsqueeze(3).broadcast_to([P, NT, UH, D]),
                                            ALU.mult).then_inc(y_part, 1)
                    dve.wait_ge(y_part, 2 * unit + s + 1)
                    nc.vector.memset(dve_idle[:], 0.0).then_inc(freed(n)[0], 1)
                elif name in ("proj0", "proj1"):
                    c = int(name[-1])
                    dve.wait_ge(xb_done, b + 1)
                    dve.wait_ge(piece_full, n + 1)
                    rows = x1[:, 2 * c:2 * c + 2, :].rearrange("p t c -> p (t c)")
                    nc.vector.tensor_tensor(rows, bank[:], rows, ALU.add).then_inc(freed(n)[0], 1)
                    if c == 1:
                        dve.wait_ge(*freed(n))
                        norm_stats(1, lambda t: x1[:, t, :], b + 1)
                elif name == "gate":
                    dve.wait_ge(*freed(n))
                    nc.vector.tensor_scalar(s_all[:, :, bass.ds(b * NT, NT)], th[:].rearrange("p t e -> p e t"),
                                            1.0, 0.5, ALU.add, ALU.mult)
                    nc.vector.tensor_scalar(z_sb[:, :, C:C + E], th[:], 1.0, 0.5, ALU.add, ALU.mult)\
                        .then_inc(expert_scores, 1)
                elif name in COL:
                    a, e = COL[name]
                    dve.wait_ge(high_done, k[0] + 1)
                    if not (isinstance(k[0], int) and k[0] < 2):
                        dve.wait_ge(low_done, k[0] - 1)
                    nc.vector.scalar_tensor_tensor(
                        out=rest[:, rest_place(name, hf)], in0=bank[:], scalar=bias[:, BIAS[name], hf:hf + 1],
                        in1=parts[:, 0, a:e], op0=ALU.add, op1=ALU.subtract).then_inc(freed(n)[0], 1)

            def batch(b, first, last):
                at = pieces(first, last)
                for g in range(UNITS):
                    ahead = not (last and g >= 2)
                    to = (b, g + 2) if g < 2 else (b + 1, g - 2)
                    for i in range(ITS):
                        for n in range(A_PER_IT):
                            gi = (g, i - 1) if i else (g - 1, ITS - 1)
                            if n == 2 and gi in at:
                                piece(at[gi], piece_number(b, first, last, *gi),
                                      *piece_args(at[gi], b, gi[0]), projection(at[gi], b, gi[0]))
                            if ahead:
                                maximum(*to, A_PER_IT * i + n)
                        if (g, i) == (0, 4) and not last:
                            dve.wait_ge(x_in, 16 * b + 32)
                            norm_stats(0, lambda t: x_sb[:, t, :], b + 2)
                    if ahead:
                        finish_maxima(*to)

            dve.wait_ge(x_in, 16)
            norm_stats(0, lambda t: x_sb[:, t, :], 1)
            nc.vector.memset(k_stack[ROWS:KROWS].rearrange("p s h n -> p (s h n)").bitcast(F32), TWO_ONES)\
                .then_inc(ones_set, 1)
            dve.wait_ge(weights_in, LOADS)
            nc.vector.tensor_tensor(bias_v[:, 2, :], bias_v[:, 0, :], bias_v[:, 1, :], ALU.add).then_inc(v_bias_done, 1)
            def first_piece(n):
                name, hf = PROLOGUE[n]
                if name in COL:
                    piece(name, n, 0, hf, 0, (len(HALF_PIECES) * hf + HALF_PIECES.index(name), hf))

            for n in range(ALONE):
                first_piece(n)
            for a in range(N_A):
                maximum(0, 0, a)
                n = piece_beside(a - READ_LATER)
                if n is not None:
                    first_piece(n)
            finish_maxima(0, 0)
            piece("shift", len(PROLOGUE), 0, 0, Unit(0, 0), None)
            for a in range(N_A):
                maximum(0, 1, a)
            finish_maxima(0, 1)
            batch(0, True, False)
            with dve.Fori(1, B - 1) as b:
                batch(b, False, False)
            batch(B - 1, False, True)
            for n, name in enumerate(EPILOGUE):
                piece(name, END + n, B - 1, 0, Unit(B - 1, UNITS - 1), None)

        @block.gpsimd
        def _(pool):
            idle = itertools.cycle(range(1, 17))

            def hold():
                c = next(idle)
                nc.gpsimd.tensor_tensor(pool_idle[:, c:c + 1], pool_idle[:, 0:1], pool_idle[:, 0:1], ALU.add)

            def normalize(which, dst, src, count):
                pool.wait_ge(mv_done[which], count)
                hold()
                nc.gpsimd.tensor_scalar(rstd[:, which], mean_var[:, which, :, 1], EPS, None, ALU.add)\
                    .then_inc(rstd_step[which], 1)
                pool.wait_ge(rstd_step[which], 2 * count - 1)
                nc.gpsimd.tensor_tensor(rstd[:, which], rstd[:, which], minus_half[:], ALU.pow)\
                    .then_inc(rstd_step[which], 1)
                pool.wait_ge(rstd_step[which], 2 * count)
                hold()
                for t in range(NT):
                    nz = nc.gpsimd.tensor_scalar(dst(t), src(t), mean_var[:, which, t, 0:1], rstd[:, which, t:t + 1],
                                                 ALU.subtract, ALU.mult)
                nz.then_inc(ln_done[which], 1)

            def split(name, n, hf, k):
                a, e = COL[name]
                src = rest[:, rest_place(name, hf)]
                pool.wait_ge(*freed(n))
                hold()
                nc.gpsimd.tensor_copy(parts[:, 1, a:e], src).then_inc(mid_done, 1)
                pool.wait_ge(mid_done, k + 1)
                nc.gpsimd.tensor_tensor(parts[:, 2, a:e], src, parts[:, 1, a:e], ALU.subtract).then_inc(low_done, 1)

            def residual(n):
                pool.wait_ge(xr_in, 16 * n + 16)
                for t in range(NT):
                    xb = nc.gpsimd.tensor_tensor(x1[:, t, :], x1[:, t, :], bias_p[:], ALU.add)
                xb.then_inc(xb_done, 1)

            def second_norm(n):
                normalize(1, lambda t: z_sb[:, t, 0:C], lambda t: x1[:, t, :], n + 1)
                pool.wait_ge(ln_done[1], n + 1)
                nc.gpsimd.tensor_tensor(x1[:], x1[:], z_sb[:, :, 0:C], ALU.add).then_inc(base_done, 1)

            def add_heads(n, unit):
                g = unit_group(unit)
                y = y_sb[:, :, g * UH * D:(g + 1) * UH * D]
                pool.wait_ge(*freed(n))
                nc.gpsimd.tensor_tensor(y, y, y_add[:].rearrange("p t h d -> p t (h d)"), ALU.add).then_inc(y_done, 1)

            def mask(b, g, i):
                q0 = score_span(i)[0]
                for p in range(2):
                    pool.wait_ge(exp_done, N_EXP * (UNITS * b + g) + 2 * i + p + 1)
                    hold()
                    tile = probs[:, i % 2 * 2 + p, :, q0:q0 + P]
                    nc.gpsimd.affine_select(out=tile, in_=tile, pattern=[[0, 2], [1, P]], compare_op=ALU.is_ge,
                                            fill=0.0, base=0, channel_multiplier=-1).then_inc(mask_done, 1)

            def batch(b, first, last):
                at = pieces(first, last)
                for g in range(UNITS):
                    if (g, 0) == (2, 0) and not first:
                        second_norm(b - 1)
                    for i in range(ITS):
                        if i >= CROSS_IT:
                            mask(b, g, i)
                        gi = (g, i - 1) if i else (g - 1, ITS - 1)
                        if gi in at:
                            name, n = at[gi], piece_number(b, first, last, *gi)
                            if name == "out_self":
                                add_heads(n, piece_args(name, b, gi[0])[2])
                            elif name in COL:
                                split(name, n, piece_args(name, b, gi[0])[1], projection(name, b, gi[0])[0])
                        if (g, i) == (0, 5) and not last:
                            normalize(0, lambda t: x_sb[:, t, :], lambda t: x_sb[:, t, :], b + 2)
                        if (g, i) == (0, 6) and not first:
                            residual(b - 1)

            nc.gpsimd.memset(ident[:], 0.0)
            nc.gpsimd.memset(causal[:], 0.0)
            nc.gpsimd.memset(minus_half[:], -0.5)
            nc.gpsimd.memset(pool_idle[:], 0.0).then_inc(pool_set, 1)
            pool.wait_ge(pool_set, 1)
            nc.gpsimd.affine_select(out=ident[:], in_=ident[:], compare_op=ALU.not_equal, fill=1.0, base=0,
                                    pattern=[[-1, P]], channel_multiplier=1).then_inc(consts, 1)
            nc.gpsimd.affine_select(out=ident_16[:], in_=causal[:], compare_op=ALU.not_equal, fill=1.0, base=0,
                                    pattern=[[-1, P]], channel_multiplier=1).then_inc(consts, 1)
            pool.wait_ge(consts, 2)
            nc.gpsimd.affine_select(out=causal[:], in_=causal[:], compare_op=ALU.is_ge, fill=NEG,
                                    base=0, pattern=[[-1, P]], channel_multiplier=1).then_inc(consts, 1)
            nc.gpsimd.memset(v_self[:], 1.0)
            nc.gpsimd.memset(v_cross[:], 1.0).then_inc(consts, 1)
            normalize(0, lambda t: x_sb[:, t, :], lambda t: x_sb[:, t, :], 1)
            for n, (name, hf) in enumerate(PROLOGUE):
                if name in COL:
                    split(name, n, hf, 5 * hf + HALF_PIECES.index(name))
            batch(0, True, False)
            with pool.Fori(1, B - 1) as b:
                batch(b, False, False)
            batch(B - 1, False, True)
            add_heads(END, Unit(B - 1, UNITS - 1))
            residual(B - 1)
            second_norm(B - 1)


FF_PROLOGUE_ITEMS = 7
FF_ITEMS = 14


def feed_forward(nc, w, z_rows, out, s_all):
    E, F, C = w["fc1s"].shape
    NTOK = z_rows.shape[0] * z_rows.shape[1]
    W_ROW = z_rows.shape[2]
    K = NTOK // E
    TILES = NTOK // P
    KT, FT, NT = C // P, F // P, K // P
    assert C == 2 * P and K == 512
    TESTS = 3
    ROUNDS = 13
    z_flat = z_rows.rearrange("b t c -> (b t) c")
    out_flat = out.rearrange("b t c -> (b t) c")

    with ExitStack() as stack:
        def sb(name, shape, dt=F32):
            return stack.enter_context(nc.sbuf_tensor(name, shape, dt))

        def ps(name, shape):
            return stack.enter_context(nc.psum_tensor(name, shape, F32))

        def sem(name):
            return stack.enter_context(nc.semaphore(name))

        w1_n = sb("w1_n", [P, FT, C]); w2_n = sb("w2_n", [P, KT, F])
        w1T = sb("w1T", [P, KT, F]); w2T = sb("w2T", [P, FT, C])
        b1_n = sb("b1_n", [E * FT, P]); b1T = sb("b1T", [P, E * FT])
        b2 = sb("b2", [P, C])
        gamma = sb("gamma", [P, KT]); beta = sb("beta", [P, KT])
        rows = sb("rows", [P, NT, W_ROW])
        y = sb("y", [P, NT, C])
        yT = sb("ff_yT", [P, KT, K])
        h = sb("h", [P, FT, K])
        o = sb("o", [P, NT, C])
        weight = sb("weight", [P, NT])
        stats = sb("ff_stats", [P, NT, 6]); mean_var = sb("ff_mv", [P, NT, 2]); rstd = sb("ff_rstd", [P, NT])
        minus_half = sb("ff_minus_half", [P, NT])
        pool_idle = sb("ff_pool_idle", [P, 17]); dve_idle = sb("ff_dve_idle", [P, 1])
        ident = sb("ff_ident", [P, P])
        ones = sb("ones", [P, P], BF16); upto = sb("upto", [P, P], BF16)
        iota = sb("iota", [P, P], BF16)
        token = sb("token", [P, 2, TILES], BF16)
        low = sb("low", [P, E]); levels = sb("levels", [P, 1 + TESTS, E]); steps = sb("steps", [P, 1 + TESTS, E])
        counts = sb("counts", [P, 1 + TESTS, E]); passed = sb("passed", [P, 1 + TESTS, E])
        reached = sb("reached", [P, TESTS, E, TILES], BF16)
        count = sb("count", [P, E])
        above = sb("above", [P, E, TILES], BF16); tied = sb("tied", [P, E, TILES], BF16)
        chosen = sb("chosen", [P, E, TILES], BF16)
        not_first = sb("not_first", [P, E, TILES]); scan = sb("scan", [P, E, TILES])
        place = sb("place", [P, E, TILES]); tmp = sb("tmp", [P, E, TILES])
        room = sb("room", [P, E]); thr = sb("thr", [P, E])
        e_place = sb("e_place", [P, TILES]); e_col = sb("e_col", [P, 4, TILES]); e_row = sb("e_row", [P, TILES])
        onehot = sb("onehot", [P, ONEHOTS, P], BF16)
        e_rhs = sb("e_rhs", [P, TILES, 2, NT], BF16)
        e_list = sb("e_list", [P, 2 * NT])
        index_next = sb("index_next", [P, NT], I32); index = sb("index", [P, NT], I32)

        h_ps = ps("h_ps", [P, 2, K])
        o_ps = ps("o_ps", [P, 2, 512])
        transpose_ps = ps("transpose_ps", [P, 2, 512])
        count_ps = ps("count_ps", [P, 2, E * TILES])
        list_ps = ps("list_ps", [P, 512])

        BANK = 512
        reached_ps = h_ps[:].rearrange("p b n -> p (b n)")[:, 0:TESTS * E * TILES]

        w1_in = sem("w1_in"); w2_in = sem("w2_in"); b2_in = sem("b2_in"); small_in = sem("small_in")
        consts = sem("ff_consts"); pool_set = sem("ff_pool_set")
        tested = sem("tested"); counted = sem("counted"); round_step = sem("round_step")
        route = sem("route"); route_ps = sem("route_ps")
        item_full = sem("item_full"); item_free = sem("item_free")
        list_step = sem("list_step"); onehot_ready = sem("onehot_ready"); onehot_used = sem("onehot_used")
        list_full = sem("list_full")
        rows_in = sem("rows_in"); stats_done = sem("ff_stats_done"); mv_done = sem("ff_mv_done")
        rstd_step = sem("ff_rstd_step"); y_done = sem("ff_y_done")
        expert_set = sem("expert_set")
        h_full = sem("h_full"); h_done = sem("h_done")
        o_full = sem("o_full"); o_biased = sem("o_biased"); o_done = sem("o_done")
        added = sem("added")

        block = stack.enter_context(nc.Block())

        @block.sync
        def _(sp):
            def load_w1(e):
                sp.dma_start(w1_n[:], w["fc1s"][e].rearrange("(t p) c -> p t c", p=P)).then_inc(w1_in, 16)

            def load_w2(e):
                sp.dma_start(w2_n[:], w["fc2s"][e].rearrange("(t p) f -> p t f", p=P)).then_inc(w2_in, 16)

            def load_b2(e):
                sp.dma_start(b2[:], w["b2s"][bass.ds(e, 1), :].broadcast_to([P, C])).then_inc(b2_in, 16)

            def expert(e, last):
                nxt = e + 1 if isinstance(e, int) else sp.snap(e + 1)
                if not last:
                    sp.wait_ge(item_free, FF_PROLOGUE_ITEMS - KT + FF_ITEMS * e)
                    load_w1(nxt)
                    sp.wait_ge(item_free, FF_PROLOGUE_ITEMS + FF_ITEMS * e + FT)
                    load_w2(nxt)
                    sp.wait_ge(o_biased, NT * e + NT)
                    load_b2(nxt)

            load_w1(0)
            load_w2(0)
            load_b2(0)
            sp.dma_start(b1_n[:], w["b1s"].rearrange("e (t p) -> (e t) p", p=P)).then_inc(small_in, 16)
            for name, tile in (("ln_gamma", gamma), ("ln_beta", beta)):
                sp.dma_start(tile[:], w[name].rearrange("(t p) -> p t", p=P),
                             allow_slow_non_contiguous=True).then_inc(small_in, 16)
            with sp.Fori(0, E - 1) as e:
                expert(e, False)

        @block.tensor
        def _(pe):
            def item(n, j, pairs):
                if not (isinstance(n, int) and n < 2):
                    pe.wait_ge(item_free, n - 1)
                bank = j % 2
                for (a, src) in pairs:
                    k = src.shape[0]
                    mm = pe.transpose(transpose_ps[:, bank, a:a + k], src, ident[0:k, 0:k])
                mm.then_inc(item_full, 1)

            def item_w1(n, j, e, t):
                if t == 0:
                    pe.wait_ge(w1_in, 16 * e + 16)
                item(n, j, [((2 * k + f) * P, w1_n[:, 2 * t + f, k * P:(k + 1) * P])
                               for k in range(KT) for f in range(2)])

            def item_w2(n, j, e, f):
                if f == 0:
                    pe.wait_ge(w2_in, 16 * e + 16)
                item(n, j, [(k * P, w2_n[:, k, f * P:(f + 1) * P]) for k in range(KT)])

            def item_y(n, j, e, k):
                pe.wait_ge(y_done, e + 1)
                item(n, j, [(t * P, y[:, t, k * P:(k + 1) * P]) for t in range(NT)])

            def list_products(e, tiles=range(TILES)):
                for t in tiles:
                    pe.wait_ge(onehot_ready, TILES * e + t + 1)
                    mm = pe.matmul(list_ps[:, 0:2 * NT], onehot[:, t % ONEHOTS], e_rhs[:, t].rearrange("p v c -> p (v c)"),
                                   start=t == 0, stop=t == TILES - 1)
                    mm.then_inc(onehot_used, 1)

            def expert(e, last):
                n0 = FF_PROLOGUE_ITEMS + FF_ITEMS * e
                for f in range(FT):
                    if f == 0:
                        pe.wait_ge(item_free, n0)
                    if f >= 2:
                        pe.wait_ge(h_done, FT * e + f - 1)
                    for k in range(KT):
                        mm = pe.matmul(h_ps[:, f % 2], w1T[:, k, f * P:(f + 1) * P], yT[:, k, :],
                                       start=k == 0, stop=k == KT - 1)
                    mm.then_inc(h_full, 1)
                    item_w2(n0 + f, f + 1, e, f)
                    if not last and f:
                        list_products(e + 1, list_tiles(f - 1))
                pe.wait_ge(item_free, n0 + FT)
                pe.wait_ge(h_done, FT * e + FT)
                for t in range(NT):
                    if t >= 2:
                        pe.wait_ge(o_biased, NT * e + t - 1)
                    for f in range(FT):
                        mm = pe.matmul(o_ps[:, t % 2, 0:C], h[:, f, t * P:(t + 1) * P], w2T[:, f, :],
                                       start=f == 0, stop=f == FT - 1)
                    mm.then_inc(o_full, 1)
                    if not last:
                        item_w1(n0 + FT + t, FT + t + 1, e + 1, t)
                if not last:
                    for k in range(KT):
                        item_y(n0 + FT + NT + k, FT + NT + k + 1, e + 1, k)

            pe.wait_ge(consts, 3)
            with pe.Fori(0, ROUNDS) as r:
                pe.wait_ge(tested, r + 1)
                flat = reached[:].rearrange("p n e t -> p (n e t)")
                pe.matmul(reached_ps[:, 0:BANK], ones[:], flat[:, 0:BANK], start=True, stop=True)
                pe.matmul(reached_ps[:, BANK:], ones[:], flat[:, BANK:], start=True, stop=True).then_inc(counted, 1)
            pe.wait_ge(route, 2)
            pe.matmul(count_ps[:, 0, :], ones[:], above[:].rearrange("p e t -> p (e t)"), start=True, stop=True)\
                .then_inc(route_ps, 1)
            pe.wait_ge(route, 4)
            for n, tile in enumerate((tied, chosen)):
                flat = tile[:].rearrange("p e t -> p (e t)")
                if n:
                    pe.wait_ge(route, CHOSEN_STEP)
                pe.matmul(count_ps[:, 0, :], upto[:], flat, start=True, stop=True)
                pe.matmul(count_ps[:, 1, :], ones[:], flat, start=True, stop=True).then_inc(route_ps, 1)
            pe.wait_ge(small_in, 48)
            item(0, 0, [(0, b1_n[:])])
            for t in range(NT):
                item_w1(1 + t, 1 + t, 0, t)
            list_products(0)
            for k in range(KT):
                item_y(1 + NT + k, 1 + NT + k, 0, k)
            with pe.Fori(0, E - 1) as e:
                expert(e, False)
            expert(E - 1, True)

        @block.scalar
        def _(act):
            def expert(e):
                for f in range(FT):
                    act.wait_ge(h_full, FT * e + f + 1)
                    nc.scalar.activation(h[:, f, :], h_ps[:, f % 2], ACT.Gelu_apprx_tanh, bias=b1T[:, bass.ds(e * FT + f, 1)])\
                        .then_inc(h_done, 1)

            act.preload_act_table(ACT.Gelu_apprx_tanh)
            act.wait_ge(item_free, 1)
            with act.Fori(0, E) as e:
                expert(e)

        @block.vector
        def _(dve):
            def free_item(n, e, dst, src, scale=None):
                dve.wait_ge(item_full, n + 1)
                if scale is None:
                    nc.vector.tensor_copy(dst, src).then_inc(item_free, 1)
                else:
                    nc.vector.tensor_scalar(dst, src, *scale, ALU.mult, ALU.add).then_inc(item_free, 1)

            def item_w1(n, j, e, t):
                src = transpose_ps[:, j % 2].rearrange("p (k f) -> p k f", k=KT)
                free_item(n, e, w1T[:, :, 2 * t * P:(2 * t + 2) * P], src)

            def item_w2(n, j, e, f):
                free_item(n, e, w2T[:, f, :], transpose_ps[:, j % 2, 0:C])

            def item_y(n, j, e, k):
                free_item(n, e, yT[:, k, :], transpose_ps[:, j % 2], (gamma[:, k:k + 1], beta[:, k:k + 1]))

            def list_head(e):
                s = LIST_STEPS * e
                if not (isinstance(e, int) and e == 0):
                    dve.wait_ge(list_full, 2 * e)
                nc.vector.tensor_copy(e_place[:], place[:, bass.ds(e, 1), :].rearrange("p o t -> p (o t)"))\
                    .then_inc(list_step, 1)
                dve.wait_ge(list_step, s + 1)
                for c in range(1, NT):
                    st = nc.vector.tensor_scalar(e_col[:, c, :], e_place[:], c * P - 0.5, None, ALU.is_ge)
                st.then_inc(list_step, 1)
                dve.wait_ge(list_step, s + 2)
                nc.vector.tensor_scalar(e_col[:, 0, :], e_place[:], -0.5, None, ALU.is_ge)
                nc.vector.scalar_tensor_tensor(out=e_row[:], in0=e_col[:, 1, :], scalar=-float(P), in1=e_place[:],
                                               op0=ALU.mult, op1=ALU.add).then_inc(list_step, 1)
                for c in range(2, NT):
                    dve.wait_ge(list_step, s + c + 1)
                    nc.vector.scalar_tensor_tensor(out=e_row[:], in0=e_col[:, c, :], scalar=-float(P), in1=e_row[:],
                                                   op0=ALU.mult, op1=ALU.add).then_inc(list_step, 1)
                dve.wait_ge(list_step, s + NT + 1)
                for c in range(NT - 1):
                    st = nc.vector.tensor_tensor(e_col[:, c, :], e_col[:, c, :], e_col[:, c + 1, :], ALU.subtract)\
                        .then_inc(list_step, 1)
                    dve.wait_ge(list_step, s + NT + 2 + c)
                for v in range(2):
                    for c in range(NT):
                        st = nc.vector.tensor_tensor(e_rhs[:, :, v, c], e_col[:, c, :], token[:, v, :], ALU.mult)
                st.then_inc(list_step, 1)
                dve.wait_ge(list_step, s + 2 * NT + 1)

            def onehots(e, tiles=range(TILES)):
                for t in tiles:
                    if not (isinstance(e, int) and e == 0 and t < ONEHOTS):
                        dve.wait_ge(onehot_used, TILES * e + t - ONEHOTS + 1)
                    nc.vector.tensor_scalar(onehot[:, t % ONEHOTS], iota[:], e_row[:, t:t + 1], None, ALU.is_equal)\
                        .then_inc(onehot_ready, 1)

            def list_tail(e):
                dve.wait_ge(onehot_used, TILES * e + TILES)
                nc.vector.tensor_copy(e_list[:], list_ps[:, 0:2 * NT]).then_inc(list_full, 1)
                dve.wait_ge(list_full, 2 * e + 1)
                if not (isinstance(e, int) and e == 0):
                    dve.wait_ge(expert_set, e)
                nc.vector.scalar_tensor_tensor(out=index_next[:], in0=e_list[:, 0:NT], scalar=float(P),
                                               in1=e_list[:, NT:2 * NT], op0=ALU.mult, op1=ALU.add)\
                    .then_inc(list_full, 1)

            def norm_stats(e):
                dve.wait_ge(rows_in, 16 * NT * (e + 1))
                for t in range(NT):
                    st = nc.vector.bn_stats(stats[:, t, :], rows[:, t, 0:C])
                st.then_inc(stats_done, 1)
                dve.wait_ge(stats_done, e + 1)
                nc.vector.memset(dve_idle[:], 0.0)
                for t in range(NT):
                    ag = nc.vector.bn_aggr(mean_var[:, t, :], stats[:, t, :])
                ag.then_inc(mv_done, 1)

            def normalize(e):
                dve.wait_ge(rstd_step, 2 * e + 2)
                for t in range(NT):
                    nz = nc.vector.tensor_scalar(y[:, t, :], rows[:, t, 0:C], mean_var[:, t, 0:1], rstd[:, t:t + 1],
                                                 ALU.subtract, ALU.mult)
                nz.then_inc(y_done, 1)

            def take_over(e):
                if not (isinstance(e, int) and e == 0):
                    dve.wait_ge(added, 16 * NT * e)
                dve.wait_ge(rows_in, 16 * NT * (e + 1))
                nc.vector.tensor_copy(index[:], index_next[:])
                nc.vector.tensor_copy(weight[:], rows[:, :, bass.ds(e + C, 1)].rearrange("p t o -> p (t o)"))\
                    .then_inc(expert_set, 1)

            def expert(e, last):
                n0 = FF_PROLOGUE_ITEMS + FF_ITEMS * e
                if not last:
                    list_head(e + 1)
                for f in range(FT):
                    item_w2(n0 + f, f + 1, e, f)
                    if not last:
                        onehots(e + 1, list_tiles(f))
                    if f == TAKE_OVER_AT:
                        take_over(e)
                    if not last and f == LIST_ITEMS:
                        list_tail(e + 1)
                for t in range(NT):
                    dve.wait_ge(o_full, NT * e + t + 1)
                    if t == 0:
                        dve.wait_ge(b2_in, 16 * e + 16)
                    nc.vector.tensor_tensor(o[:, t, :], o_ps[:, t % 2, 0:C], b2[:], ALU.add).then_inc(o_biased, 1)
                    dve.wait_ge(o_biased, NT * e + t + 1)
                    nc.vector.tensor_scalar(o[:, t, :], o[:, t, :], weight[:, t:t + 1], None, ALU.mult)\
                        .then_inc(o_done, 1)
                    if not last:
                        item_w1(n0 + FT + t, FT + t + 1, e + 1, t)
                        if t == NORM_AT:
                            norm_stats(e + 1)
                        if t == NORM_AT + 1:
                            normalize(e + 1)
                if not last:
                    for k in range(KT):
                        item_y(n0 + FT + NT + k, FT + NT + k + 1, e + 1, k)

            flat = lambda tile: tile[:].rearrange("p e t -> p (e t)")
            wide = lambda tile: tile[:].unsqueeze(2).broadcast_to([P, E, TILES])
            nc.vector.memset(levels[:, 0, :], 0.0)
            nc.vector.memset(counts[:, 0, :], float(K))
            for n in range(TESTS + 1):
                nc.vector.memset(steps[:, n, :], 0.5 * n)
            for n in range(1, TESTS + 1):
                init = nc.vector.memset(levels[:, n, :], 0.5 * n)
            init.then_inc(round_step, 1)
            with dve.Fori(0, ROUNDS) as r:
                dve.wait_ge(round_step, 4 * r + 1)
                nc.vector.tensor_tensor(reached[:], s_all[:].unsqueeze(1).broadcast_to([P, TESTS, E, TILES]),
                                        levels[:, 1:, :].unsqueeze(3).broadcast_to([P, TESTS, E, TILES]), ALU.is_ge)\
                    .then_inc(tested, 1)
                nc.vector.tensor_scalar(steps[:], steps[:], 0.25, None, ALU.mult)
                dve.wait_ge(counted, r + 1)
                nc.vector.tensor_reduce(counts[:, 1:, :].rearrange("p n e -> p (n e)"),
                                        reached_ps.rearrange("p (n t) -> p n t", t=TILES), AX.X, ALU.add)\
                    .then_inc(round_step, 1)
                dve.wait_ge(round_step, 4 * r + 2)
                nc.vector.scalar_tensor_tensor(out=passed[:], in0=counts[:], scalar=K - 0.5, in1=levels[:],
                                               op0=ALU.is_ge, op1=ALU.mult).then_inc(round_step, 1)
                dve.wait_ge(round_step, 4 * r + 3)
                nc.vector.tensor_reduce(low[:], passed[:].rearrange("p n e -> p e n"), AX.X, ALU.max)\
                    .then_inc(round_step, 1)
                dve.wait_ge(round_step, 4 * r + 4)
                nc.vector.tensor_tensor(levels[:], low[:].unsqueeze(1).broadcast_to([P, 1 + TESTS, E]), steps[:],
                                        ALU.add).then_inc(round_step, 1)
            nc.vector.tensor_copy(thr[:], low[:]).then_inc(route, 1)
            dve.wait_ge(route, 1)
            nc.vector.tensor_tensor(above[:], s_all[:], wide(thr), ALU.is_gt).then_inc(route, 1)
            nc.vector.tensor_tensor(tied[:], s_all[:], wide(thr), ALU.is_equal).then_inc(route, 1)
            dve.wait_ge(route_ps, 1)
            nc.vector.tensor_reduce(count[:], count_ps[:, 0, :].rearrange("p (e t) -> p e t", e=E), AX.X, ALU.add)\
                .then_inc(route, 1)
            dve.wait_ge(route, 4)
            nc.vector.tensor_scalar(room[:], count[:], -1.0, float(K), ALU.mult, ALU.add).then_inc(route, 1)
            nc.vector.memset(not_first[:], 1.0).then_inc(route, 1)
            dve.wait_ge(route, 6)
            nc.vector.memset(not_first[:, :, 0:1], 0.0).then_inc(route, 1)
            dve.wait_ge(route, 7)

            def ranks(step, n):
                dve.wait_ge(route_ps, n)
                nc.vector.tensor_tensor_scan(flat(scan), flat(not_first), count_ps[:, 1, :], 0.0, ALU.mult, ALU.add)\
                    .then_inc(route, 1)
                dve.wait_ge(route, step + 1)
                nc.vector.tensor_tensor(flat(tmp), flat(scan), count_ps[:, 1, :], ALU.subtract).then_inc(route, 1)
                dve.wait_ge(route, step + 2)
                nc.vector.tensor_tensor(flat(place), flat(tmp), count_ps[:, 0, :], ALU.add).then_inc(route, 1)
                dve.wait_ge(route, step + 3)

            ranks(7, 2)
            nc.vector.tensor_tensor(tmp[:], place[:], wide(room), ALU.is_le).then_inc(route, 1)
            dve.wait_ge(route, 11)
            nc.vector.tensor_tensor(tmp[:], tmp[:], tied[:], ALU.mult).then_inc(route, 1)
            dve.wait_ge(route, 12)
            nc.vector.tensor_tensor(chosen[:], tmp[:], above[:], ALU.add).then_inc(route, 1)
            ranks(CHOSEN_STEP, 3)
            nc.vector.tensor_tensor(tmp[:], place[:], chosen[:], ALU.mult).then_inc(route, 1)
            dve.wait_ge(route, 17)
            nc.vector.tensor_scalar(place[:], tmp[:], -1.0, None, ALU.add).then_inc(route, 1)
            dve.wait_ge(route, 18)
            dve.wait_ge(consts, 3)
            dve.wait_ge(item_full, 1)
            nc.vector.tensor_copy(b1T[:], transpose_ps[:, 0, 0:E * FT]).then_inc(item_free, 1)
            for t in range(NT):
                item_w1(1 + t, 1 + t, 0, t)
            list_head(0)
            onehots(0)
            list_tail(0)
            norm_stats(0)
            normalize(0)
            dve.wait_ge(small_in, 48)
            for k in range(KT):
                item_y(1 + NT + k, 1 + NT + k, 0, k)
            expert(0, False)
            with dve.Fori(1, E - 1) as e:
                expert(e, False)
            expert(E - 1, True)

        @block.gpsimd
        def _(pool):
            idle = itertools.cycle(range(1, 17))

            def hold():
                c = next(idle)
                nc.gpsimd.tensor_tensor(pool_idle[:, c:c + 1], pool_idle[:, 0:1], pool_idle[:, 0:1], ALU.add)

            def gather(e):
                pool.wait_ge(list_full, 2 * e + 2)
                if not (isinstance(e, int) and e == 0):
                    pool.wait_ge(expert_set, e)
                hold()
                for t in range(NT):
                    pool.indirect_dma_start(
                        out=rows[:, t, :], out_offset=None, in_=z_flat,
                        in_offset=bass.IndirectOffsetOnAxis(ap=index_next[:, t:t + 1].bitcast(U32), axis=0))\
                        .then_inc(rows_in, 16)

            def reciprocal_deviation(e):
                pool.wait_ge(mv_done, e + 1)
                hold()
                nc.gpsimd.tensor_scalar(rstd[:], mean_var[:, :, 1], EPS, None, ALU.add).then_inc(rstd_step, 1)
                pool.wait_ge(rstd_step, 2 * e + 1)
                nc.gpsimd.tensor_tensor(rstd[:], rstd[:], minus_half[:], ALU.pow).then_inc(rstd_step, 1)

            def scatter(e):
                for t in range(NT):
                    pool.wait_ge(o_done, NT * e + t + 1)
                    hold()
                    pool.indirect_dma_start(
                        out=out_flat, out_offset=bass.IndirectOffsetOnAxis(ap=index[:, t:t + 1].bitcast(U32), axis=0),
                        in_=o[:, t, :], in_offset=None, compute_op=ALU.add).then_inc(added, 16)

            nc.gpsimd.memset(ident[:], 0.0)
            nc.gpsimd.memset(ones[:], 1.0)
            nc.gpsimd.memset(upto[:], 1.0)
            nc.gpsimd.memset(minus_half[:], -0.5)
            nc.gpsimd.memset(pool_idle[:], 0.0).then_inc(pool_set, 1)
            pool.wait_ge(pool_set, 1)
            nc.gpsimd.affine_select(out=ident[:], in_=ident[:], compare_op=ALU.not_equal, fill=1.0, base=0,
                                    pattern=[[-1, P]], channel_multiplier=1).then_inc(consts, 1)
            nc.gpsimd.affine_select(out=upto[:], in_=upto[:], compare_op=ALU.is_ge, fill=0.0, base=0,
                                    pattern=[[1, P]], channel_multiplier=-1).then_inc(consts, 1)
            nc.gpsimd.iota(iota[:], pattern=[[1, P]], base=0, channel_multiplier=0, allow_small_or_imprecise_dtypes=True)
            nc.gpsimd.iota(token[:, 0, :], pattern=[[1, TILES]], base=0, channel_multiplier=0,
                           allow_small_or_imprecise_dtypes=True)
            nc.gpsimd.iota(token[:, 1, :], pattern=[[0, TILES]], base=0, channel_multiplier=1,
                           allow_small_or_imprecise_dtypes=True).then_inc(consts, 1)
            gather(0)
            reciprocal_deviation(0)
            with pool.Fori(0, E - 1) as e:
                gather(e + 1)
                reciprocal_deviation(e + 1)
                scatter(e)
            scatter(E - 1)
            pool.wait_ge(added, 16 * NT * E)


CHOSEN_STEP = 13
ONEHOTS = 12
LIST_ITEMS = 6
TAKE_OVER_AT = 4
NORM_AT = 1


def list_tiles(f, tiles=32):
    each = -(-tiles // LIST_ITEMS)
    return range(min(f * each, tiles), min((f + 1) * each, tiles))

LIST_STEPS = 2 * 4 + 1


def kernel(**inputs):
    import numpy as np
    import concourse.bacc as bacc
    from concourse.bass_utils import run_bass_kernel_spmd

    nc = bacc.Bacc("TRN2", target_bir_lowering=False, num_devices=1)
    arrays, ins, w = {}, {}, {}
    for name in inputs:
        a = np.ascontiguousarray(inputs[name])
        arrays[f"in_{name}"] = a
        ins[name] = nc.dram_tensor(f"in_{name}", a.shape, mybir.dt.from_np(a.dtype), kind="ExternalInput").ap()
        if name.startswith("L0_"):
            w[name.split("_", 2)[2]] = ins[name]
    shape = inputs["x"].shape
    out = nc.dram_tensor("out", shape, F32, kind="ExternalOutput").ap()
    program(nc, ins["x"], ins["ctx_512"], w, out)
    r = run_bass_kernel_spmd(nc, [arrays], core_ids=[0])
    return r.results[0]["out"]


def program(nc, x, ctx_in, w, out, z_rows=None):
    B, T, C = x.shape
    E = w["gate_w"].shape[0]
    if z_rows is None:
        z_rows = nc.dram_tensor("z_rows", (B, T, C + E), F32).ap()
    parts_dram = nc.dram_tensor("parts_dram", (2, 3, P, Q_COLS + K_COLS), BF16).ap()
    shift_dram = nc.dram_tensor("shift_dram", (2, SHIFT_ROWS, UH * Q_COLS), BF16).ap()
    with nc.sbuf_tensor("s_all", [P, E, B * T // P], F32) as s_all:
        attention(nc, x, ctx_in, w, z_rows, out, parts_dram, shift_dram, s_all)
        feed_forward(nc, w, z_rows, out, s_all)
```
